# Optimizing a Trainium2 kernel written in Bass

```python
import numpy as np
import jax
import jax.numpy as jnp

def _softmax(x, axis=-1):
    return jax.nn.softmax(x, axis=axis)
def _gelu(x):
    return jax.nn.gelu(x, approximate=True)
def _silu(x):
    return jax.nn.silu(x)
def _sigmoid(x):
    return jax.nn.sigmoid(x)
def _layernorm(x, axis=-1, eps=1e-5):
    m = jnp.mean(x, axis=axis, keepdims=True)
    v = jnp.var(x, axis=axis, keepdims=True)
    return (x - m) / jnp.sqrt(v + eps)
def _scatter_add(tgt, idx, src, axis=0):
    return tgt.at[idx].add(src)
def _segment_sum(src, seg, n):
    return jax.ops.segment_sum(src, seg, n)

kernel_name = 'mk_conv_preact_d2_conv_nchw16_c7ac28'

def setup_inputs(seed: int = 0):
    np.random.seed(seed)
    _w = jnp.asarray
    def _rec_inputs():
        import jax
        import jax.numpy as jnp
        _gk = jax.random.key(seed)
        x = -0.000125 + 0.9999 * jax.random.normal(jax.random.fold_in(_gk, 1), (8, 16, 512, 512), jnp.float32)
        return x
    x = _rec_inputs()
    def _L0_conv_setup():
        import jax, jax.numpy as jnp
        import numpy as np
        from jax import lax
        K = 3
        P = 1
        _CONV_PAD = K - 1 - P

        def _rconv(a, w):
            return lax.conv_general_dilated(a, w, window_strides=(1, 1), padding=[(_CONV_PAD, _CONV_PAD), (_CONV_PAD, _CONV_PAD)], dimension_numbers=('NCHW', 'OIHW', 'NCHW'))
        key = jax.random.key(seed)
        k1, k2, k3, k4, k5 = jax.random.split(key, 5)
        N, C_IN, C_OUT, H, W = (8, 16, 16, 512, 512)
        x = jax.random.normal(k1, (N, C_IN, H, W), dtype=jnp.float32)
        scale = 1.0 / np.sqrt(C_IN * K * K)
        w_real = jax.random.normal(k2, (C_IN, C_OUT, K, K), dtype=jnp.float32) * scale
        w_imag = jax.random.normal(k3, (C_IN, C_OUT, K, K), dtype=jnp.float32) * scale
        b_real = jax.random.normal(k4, (C_OUT,), dtype=jnp.float32) * scale
        b_imag = jax.random.normal(k5, (C_OUT,), dtype=jnp.float32) * scale
        return {'x': x, 'w_real': w_real, 'w_imag': w_imag, 'b_real': b_real, 'b_imag': b_imag}
    _L0_conv_all = _L0_conv_setup()
    _L0_conv_in = {k: v for k, v in _L0_conv_all.items() if k in ('w_real', 'w_imag', 'b_real', 'b_imag', )}
    del _L0_conv_all

    def _L1_conv_setup():
        import jax, jax.numpy as jnp
        import numpy as np
        from jax import lax
        KERNEL_SIZE = 15

        def _mean_filter(x, k):
            B, C, H, W = x.shape
            pad = k // 2
            kh = jnp.ones((1, 1, k, 1), x.dtype) / k
            kw = jnp.ones((1, 1, 1, k), x.dtype) / k
            xr = x.reshape(B * C, 1, H, W)
            y = lax.conv_general_dilated(xr, kh, (1, 1), [(pad, pad), (0, 0)])
            y = lax.conv_general_dilated(y, kw, (1, 1), [(0, 0), (pad, pad)])
            return y.reshape(B, C, H, W)
        key = jax.random.key(seed)
        x = jax.random.normal(key, (8, 16, 512, 512), dtype=jnp.float32)
        return {'x': x}
    _L1_conv_all = _L1_conv_setup()
    _L1_conv_in = {k: v for k, v in _L1_conv_all.items() if k in ()}
    del _L1_conv_all

    return {
        "x": x,
        "L0_conv_w_real": _L0_conv_in["w_real"],
        "L0_conv_w_imag": _L0_conv_in["w_imag"],
        "L0_conv_b_real": _L0_conv_in["b_real"],
        "L0_conv_b_imag": _L0_conv_in["b_imag"],
    }

def reference(x, L0_conv_w_real, L0_conv_w_imag, L0_conv_b_real, L0_conv_b_imag):
    import jax
    import jax.numpy as jnp
    def _L0_conv_ref(x, w_real, w_imag, b_real, b_imag):
        import jax, jax.numpy as jnp
        import numpy as np
        from jax import lax
        K = 3
        P = 1
        _CONV_PAD = K - 1 - P

        def _rconv(a, w):
            return lax.conv_general_dilated(a, w, window_strides=(1, 1), padding=[(_CONV_PAD, _CONV_PAD), (_CONV_PAD, _CONV_PAD)], dimension_numbers=('NCHW', 'OIHW', 'NCHW'))
        X = jnp.fft.rfftn(x, axes=(-2, -1), norm='backward')
        Xr, Xi = (jnp.real(X), jnp.imag(X))
        wr = jnp.transpose(jnp.flip(w_real, axis=(-2, -1)), (1, 0, 2, 3))
        wi = jnp.transpose(jnp.flip(w_imag, axis=(-2, -1)), (1, 0, 2, 3))
        Yr = _rconv(Xr, wr) - _rconv(Xi, wi) + b_real[:, None, None]
        Yi = _rconv(Xr, wi) + _rconv(Xi, wr) + b_imag[:, None, None]
        Y = lax.complex(Yr, Yi)
        return jnp.fft.irfftn(Y, axes=(-2, -1), norm='backward')

    def _L1_conv_ref(x):
        import jax, jax.numpy as jnp
        import numpy as np
        from jax import lax
        KERNEL_SIZE = 15

        def _mean_filter(x, k):
            B, C, H, W = x.shape
            pad = k // 2
            kh = jnp.ones((1, 1, k, 1), x.dtype) / k
            kw = jnp.ones((1, 1, 1, k), x.dtype) / k
            xr = x.reshape(B * C, 1, H, W)
            y = lax.conv_general_dilated(xr, kh, (1, 1), [(pad, pad), (0, 0)])
            y = lax.conv_general_dilated(y, kw, (1, 1), [(0, 0), (pad, pad)])
            return y.reshape(B, C, H, W)
        return _mean_filter(x, KERNEL_SIZE)

    def _gn(v, G=8, eps=1e-5):
        B_, C_, H_, W_ = v.shape
        g = v.reshape(B_, G, C_ // G, H_, W_)
        m = jnp.mean(g, axis=(2, 3, 4), keepdims=True)
        s = jnp.var(g, axis=(2, 3, 4), keepdims=True)
        return ((g - m) / jnp.sqrt(s + eps)).reshape(v.shape)

    def _ln_c(v, eps=1e-6):
        m = jnp.mean(v, axis=1, keepdims=True)
        s = jnp.var(v, axis=1, keepdims=True)
        return (v - m) / jnp.sqrt(s + eps)

    def _ln_t(v, eps=1e-5):
        m = jnp.mean(v, axis=-1, keepdims=True)
        s = jnp.var(v, axis=-1, keepdims=True)
        return (v - m) / jnp.sqrt(s + eps)

    def _to_tokens(v):
        B_, C_, H_, W_ = v.shape
        return v.reshape(B_, C_, H_ * W_).transpose(0, 2, 1)
    def _from_tokens(t, like):
        B_, C_, H_, W_ = like.shape
        return t.transpose(0, 2, 1).reshape(B_, C_, H_, W_)

    x = x + _L0_conv_ref(_gn(x), L0_conv_w_real, L0_conv_w_imag, L0_conv_b_real, L0_conv_b_imag)
    x = x + _L1_conv_ref(_gn(x))
    return x


_drawn_inputs = setup_inputs


def setup_inputs(seed=0):
    import zlib

    import numpy as np

    out = dict(_drawn_inputs(seed))
    spreads = {}
    factors = {'L0_conv_b_real': 200.0, 'L0_conv_b_imag': 200.0}
    for name, (base, spread) in spreads.items():
        noise = np.random.default_rng([zlib.crc32(name.encode()), seed]).standard_normal(out[name].shape)
        drawn = base * np.exp(spread * noise) if base else spread * noise
        out[name] = jnp.asarray(drawn.astype(out[name].dtype))
    for name, factor in factors.items():
        out[name] = (out[name] * factor).astype(out[name].dtype)
    return out
```

```python
from contextlib import ExitStack

import numpy as np

import concourse.bass as bass
from concourse import mybir

F32 = mybir.dt.float32
ALU = mybir.AluOpType
ACT = mybir.ActivationFunctionType

P = 128
B, C, H, W = 8, 16, 512, 512
HB = P // C
T = H // HB
GROUP = 2 * HB
HALF = W // 2
NZ = 5
K = 15
R = K // 2
EPS = 1e-5
CHUNK = 8
NCH = T // CHUNK
PADW = K + W + R
SUMW = W + R
PRIMED = 1
NV = 3 * C
QUARTER = HALF // 4

TABLES = ["ident", "prev", "next_", "neg_ident", "neg_prev", "group_mean", "hilbert", "cosw",
          "to_virtual", "from_virtual", "hb_mask", "c_mask", "trig_h", "virt_h", "row_count", "hilbert_kernel"]


def tables():
    th = 2 * np.pi / W
    p = np.arange(P)
    c, hb = p // HB, p % HB
    h = (hb[:, None] * T + np.arange(T)[None, :])
    eye = np.eye(P)
    prev = np.zeros((P, P))
    nxt = np.zeros((P, P))
    for m in range(P):
        if m % HB != 0:
            prev[m - 1, m] = 1
        if m % HB != HB - 1:
            nxt[m + 1, m] = 1

    def kern(n):
        n = np.asarray(n)
        odd = n % 2 == 1
        return np.where(odd, 2.0 / W / np.tan(np.pi * np.where(odd, n, 1) / W), 0.0)

    hil = np.zeros((P, 4, HALF + NZ))
    for k in range(4):
        par, half = k // 2, k % 2
        w = 2 * (P * half + np.arange(P)) + par
        wo = 2 * np.arange(HALF) + (1 - par)
        hil[:, k, :HALF] = kern(wo[None, :] - w[:, None])
        hil[:, k, HALF + 0] = 2.0 / W
        hil[:, k, HALF + 1] = np.sin(th * w) / W
        hil[:, k, HALF + 2] = -np.cos(th * w) / W
        hil[:, k, HALF + 3] = -2.0 / W
        hil[:, k, HALF + 4] = -np.sin(th * w) / W
    wsep = np.stack([2 * np.arange(-QUARTER, HALF), 2 * np.arange(-QUARTER, HALF) + 1])
    tov = np.zeros((P, NV))
    fromv = np.zeros((NV, 3, P))
    for cc in range(C):
        for j in range(3):
            tov[cc * HB, j * C + cc] = 1
            fromv[j * C + cc, j, cc * HB:(cc + 1) * HB] = -1
    trig = np.stack([np.cos(th * h), np.sin(th * h)], 1)
    virt = np.stack([np.ones_like(h) / H, np.cos(th * h) / H, np.sin(th * h) / H], 2)
    count = np.minimum(h + R, H - 1) - np.maximum(h - R, 0) + 1
    out = {
        "ident": eye, "prev": prev, "next_": nxt, "neg_ident": -eye, "neg_prev": -prev,
        "group_mean": (p[:, None] // GROUP == p[None, :] // GROUP) / GROUP,
        "hilbert": hil,
        "cosw": np.broadcast_to(np.cos(th * wsep), (P, *wsep.shape)),
        "to_virtual": tov, "from_virtual": fromv,
        "hb_mask": hb[:, None] == np.arange(HB)[None, :],
        "c_mask": c[:, None] == np.arange(C)[None, :],
        "trig_h": trig, "virt_h": virt, "row_count": count,
        "hilbert_kernel": np.tile(kern(np.arange(W)), (P, 1)),
    }
    return {k: np.ascontiguousarray(v, dtype=np.float32) for k, v in out.items()}


def build(nc, x, w_real, w_imag, b_real, b_imag, tab, out):
    x_v = x.rearrange("b c (hb t) w -> (b c hb) (t w)", hb=HB)
    out_v = out.rearrange("b c (hb t) w -> (b c hb) (t w)", hb=HB)
    with ExitStack() as ctx:
        def sb(name, shape):
            return ctx.enter_context(nc.sbuf_tensor(name, shape, F32))

        def sem(name):
            return ctx.enter_context(nc.semaphore(name))

        img = sb("img", [P, T, W])
        smat = sb("smat", [P, T, 6, C])
        tb = {n: sb(n, list(tab[n].shape)) for n in TABLES if n != "hilbert_kernel"}
        bd = [sb(f"bd{s}", [P, 6, C, HB]) for s in range(2)]
        vmat = sb("vmat", [NV, 6, NV])
        uvw = [sb(f"uvw{s}", [P, 4 * 3, C]) for s in range(2)]
        rmap = sb("rmap", [P, 3, 2, HALF])
        bias_row = sb("bias_row", [P, W])
        cosw, sinw = tb["cosw"][:, :, QUARTER:], tb["cosw"][:, :, 0:HALF]
        work = sb("work", [P, 3 * W + 4 * (HALF + NZ)])
        g = [work[:, s * W:(s + 1) * W] for s in range(2)]
        xT = work[:, 2 * W:3 * W].rearrange("p (k m) -> p k m", k=4)
        hs = [work[:, 3 * W + s * 2 * (HALF + NZ):3 * W + (s + 1) * 2 * (HALF + NZ)]
              .rearrange("p (a n) -> p a n", a=2) for s in range(2)]
        padded = [work[:, s * PADW:(s + 1) * PADW] for s in range(2)]
        sums = [work[:, 2 * PADW + s * SUMW:2 * PADW + (s + 1) * SUMW] for s in range(2)]
        assert 2 * (PADW + SUMW) <= 3 * W + 4 * (HALF + NZ)
        ob = [sb(f"ob{s}", [P, 2, W]) for s in range(2)]
        t1, t2 = (ob[0][:, i, :].rearrange("p (a j) -> p a j", a=2) for i in range(2))
        wadd = [ob[1][:, i, :].rearrange("p (a j) -> p a j", a=2) for i in range(2)]
        qx = sb("qx", [P, 2, HALF])
        stat = sb("stat", [P, T, 6])
        sc = sb("sc", [P, 24])
        box_bias = sb("box_bias", [P, T])

        xt_ps = ctx.enter_context(nc.psum_tensor("xt_ps", [P, 4, P], F32))
        h_ps = ctx.enter_context(nc.psum_tensor("h_ps", [P, 2, W], F32))
        p0 = ctx.enter_context(nc.psum_tensor("p0", [P, W], F32))
        p1 = ctx.enter_context(nc.psum_tensor("p1", [P, W], F32))
        p2 = ctx.enter_context(nc.psum_tensor("p2", [P, W], F32))
        c_ps = ctx.enter_context(nc.psum_tensor("c_ps", [P, W], F32))
        uv_ps = ctx.enter_context(nc.psum_tensor("uv_ps", [P, W], F32))

        tab_in, w_in, zeroed = sem("tab_in"), sem("w_in"), sem("zeroed")
        setup_chain, setup_done = sem("setup_chain"), sem("setup_done")
        vmat_spaced, vmat_in = sem("vmat_spaced"), sem("vmat_in")
        loaded = [sem(f"loaded{k}") for k in range(NCH)]
        uvw_ready, uv_summed, rows_counted = sem("uvw_ready"), sem("uv_summed"), sem("rows_counted")
        chain = sem("chain")
        s_mean, s_gmean, s_dev, s_gvar = sem("s_mean"), sem("s_gmean"), sem("s_dev"), sem("s_gvar")
        s_var, s_sd, s_scale, s_vsc_ps, s_vscale = (sem("s_var"), sem("s_sd"), sem("s_scale"),
                                                    sem("s_vsc_ps"), sem("s_vscale"))
        vg_done, vxt_made, vxt_kept, vh_made, vh_kept = (sem("vg_done"), sem("vxt_made"), sem("vxt_kept"),
                                                         sem("vh_made"), sem("vh_kept"))
        v_mixed, v_rows, v_spread, v_maps = sem("v_mixed"), sem("v_rows"), sem("v_spread"), sem("v_maps")
        g_done, xt_made, xt_kept, h_made, h_kept = (sem("g_done"), sem("xt_made"), sem("xt_kept"),
                                                    sem("h_made"), sem("h_kept"))
        bd_ready, p1_ready, p2_ready, p0_ready = sem("bd_ready"), sem("p1_ready"), sem("p2_ready"), sem("p0_ready")
        t1_done, t2_done, q_done, q3_done = sem("t1_done"), sem("t2_done"), sem("q_done"), sem("q3_done")
        wa_done, w_done, qx_done, x1_done = sem("wa_done"), sem("w_done"), sem("qx_done"), sem("x1_done")
        bias_added, x1_counted = sem("bias_added"), sem("x1_counted")
        pads_zero, col_summed, row_padded, row_summed, row_out = (
            sem("pads_zero"), sem("col_summed"), sem("row_padded"), sem("row_summed"), sem("row_out"))
        stored = [sem(f"stored{s}") for s in range(2)]

        flat = img[:, 0:24, :].rearrange("p t w -> p (t w)")
        raw = [flat[:, i * 144:(i + 1) * 144].rearrange("p (o a b) -> p o a b", o=C, a=3) for i in range(2)]
        vraw = [flat[:, (2 + i) * 144:(3 + i) * 144].rearrange("p (o a b) -> p o a b", o=C, a=3)
                for i in range(2)]
        aa = flat[:, 1024:1024 + 288].rearrange("p (r f o b) -> p r f o b", r=2, f=3, o=C)
        base = flat[:, 1536:1536 + 288].rearrange("p (f j o) -> p f j o", f=3, j=6)
        hker = flat[:, 2048:2048 + W]
        scr = flat[:, 4096:4096 + T * C].rearrange("p (t o) -> p t o", o=C)
        spaced = flat[:, 8192:8192 + 6 * NV].rearrange("p (j m) -> p j m", j=6)
        bcol = sc[:, 20:22]

        def parity(ap):
            return ap.rearrange("p (j two) -> p two j", two=2)

        def halves(ap):
            return ap.rearrange("p (a j) -> p a j", a=2)

        block = ctx.enter_context(nc.Block())

        @block.sync
        def _(sp):
            for n in TABLES:
                dst = hker if n == "hilbert_kernel" else tb[n][:]
                sp.dma_start(dst, tab[n]).then_inc(tab_in, 16)
            sp.wait_ge(zeroed, 1)
            for i, wr in enumerate((w_real, w_imag)):
                w_flat = wr.rearrange("i o a b -> i (o a b)")
                for k in range(HB):
                    sp.dma_start(flat[k:P:HB, i * 144:(i + 1) * 144], w_flat).then_inc(w_in, 16)
                for k in range(3):
                    sp.dma_start(flat[32 * k:32 * k + C, (2 + i) * 144:(3 + i) * 144], w_flat).then_inc(w_in, 16)
            for i, br in enumerate((b_real, b_imag)):
                sp.dma_start(sc[0:P:HB, 20 + i:21 + i], br.rearrange("(c o) -> c o", o=1)).then_inc(w_in, 16)

            def load(b, k):
                sp.dma_start(img[:, k * CHUNK:(k + 1) * CHUNK, :].rearrange("p t w -> p (t w)"),
                             x_v[bass.ds(b * P, P), k * CHUNK * W:(k + 1) * CHUNK * W]).then_inc(loaded[k], 16)

            def store(b, j, s):
                sp.wait_ge(row_out, PRIMED + b * T + j * 2 + 2)
                sp.dma_start(out_v[bass.ds(b * P, P), bass.ds(j * (2 * W), 2 * W)],
                             ob[s][:].rearrange("p t w -> p (t w)")).then_inc(stored[s], 16)

            sp.wait_ge(vmat_spaced, 1)
            for k in range(3):
                sp.dma_start(vmat[k * C:(k + 1) * C, :, :].rearrange("p j m -> p (j m)"),
                             spaced[32 * k:32 * k + C, :, :].rearrange("p j m -> p (j m)")).then_inc(vmat_in, 16)
            sp.wait_ge(vmat_in, 48)
            sp.wait_ge(setup_done, 1)
            for k in [*range(1, NCH), 0]:
                load(0, k)

            with sp.Fori(0, B - 1) as b:
                with sp.Fori(0, 4) as i:
                    store(b, i * 2, 0)
                    store(b, i * 2 + 1, 1)
                for k in range(1, NCH - 1):
                    for j in range(4 * k + 4, 4 * k + 8):
                        store(b, j, j % 2)
                    sp.wait_ge(col_summed, b * T + CHUNK * (k + 1) + R + 1)
                    load(b + 1, k)
                for k in (NCH - 1, 0):
                    load(b + 1, k)
            with sp.Fori(0, T // 4) as i:
                store(B - 1, i * 2, 0)
                store(B - 1, i * 2 + 1, 1)
            for s in range(2):
                sp.wait_ge(stored[s], PRIMED + 16 * B * T // 4)

        @block.tensor
        def _(pe):
            mm = nc.tensor.matmul
            pe.wait_ge(tab_in, 16 * len(TABLES))
            pe.wait_ge(setup_done, 1)
            pe.wait_ge(vmat_in, 48)

            def group_stats(n):
                pe.wait_ge(s_mean, n)
                mm(c_ps[:, 16:17], tb["group_mean"][:], sc[:, 0:1], start=True, stop=True).then_inc(s_gmean, 1)
                pe.wait_ge(s_dev, n)
                mm(c_ps[:, 17:18], tb["group_mean"][:], sc[:, 3:4], start=True, stop=True).then_inc(s_gvar, 1)

            def hold():
                mm(xt_ps[:, 0, 0:2], tb["ident"][:], tb["ident"][:, 0:2], start=True, stop=True)

            def turn(gs, rows=P):
                for k in range(4):
                    m = nc.tensor.transpose(xt_ps[:, k, 0:rows], gs[0:rows, k * P:(k + 1) * P],
                                            tb["ident"][0:rows, 0:rows])
                return m

            def hilbert(rows=P):
                for a in range(2):
                    for half in range(2):
                        k = 2 * (1 - a) + half
                        m = mm(h_ps[0:rows, a, 0:HALF + NZ], xT[:, k, 0:rows], tb["hilbert"][:, k, :],
                               start=(half == 0), stop=(half == 1))
                return m

            def edge_terms(mats, h_row, rows):
                z = h_row[0:rows, :, HALF:HALF + NZ]
                zo = z.rearrange("p a f -> p f a")
                c = c_ps[0:rows, :]
                mm(c[:, 0:4], mats(3), zo[:, 0:2, :], start=True, stop=False, skip_group_check=True)
                mm(c[:, 2:6], mats(5), zo[:, 2:4, :], start=False, stop=False, skip_group_check=True)
                mm(c[:, 2:4], mats(2), z[:, ::-1, 2:3], start=False, stop=False, skip_group_check=True)
                mm(c[:, 2:4], mats(4), z[:, ::-1, 4:5], start=False, stop=True, skip_group_check=True)

            with pe.Fori(0, B) as b:
                for q, k in enumerate([*range(1, NCH), 0]):
                    pe.wait_ge(loaded[k], b * 16 + 16)
                    for s in range(2):
                        pe.wait_ge(uvw_ready, b * (T // 4) + (2 * q + s + 1))
                        for r in range(4):
                            row = k * CHUNK + 4 * s + r
                            m = mm(uv_ps[0:NV, :], uvw[s][:, 3 * r:3 * r + 3, :].rearrange("p j c -> p (j c)"), img[:, row, :],
                                   start=(q == 0 and s == 0 and r == 0),
                                   stop=(q == NCH - 1 and s == 1 and r == 3))
                        m.then_inc(uv_summed, 1)
                group_stats(b * 2 + 1)
                pe.wait_ge(s_scale, b * 2 + 1)
                mm(c_ps[0:NV, 18:20], tb["to_virtual"][:], sc[:, 8:10], start=True, stop=True).then_inc(s_vsc_ps, 1)

                pe.wait_ge(vg_done, b + 1)
                hold()
                turn(g[0], NV).then_inc(vxt_made, 1)
                pe.wait_ge(vxt_kept, b + 1)
                hilbert(NV).then_inc(vh_made, 1)
                pe.wait_ge(vh_kept, b + 1)
                pe.wait_ge(s_vscale, b + 1)
                hold()
                edge_terms(lambda j: vmat[:, j, :], hs[0], NV)
                for pt, jg, jh in ((p1, 2, 3), (p2, 4, 5), (p0, 0, 1)):
                    mm(pt[0:NV, :], vmat[:, jg, :], g[0][0:NV, :], start=True, stop=False)
                    m = mm(pt[0:NV, :], vmat[:, jh, :], hs[0][0:NV, :, 0:HALF], start=False, stop=True)
                m.then_inc(v_mixed, 1)
                pe.wait_ge(v_rows, b + 1)
                for j, pt in enumerate((p0, p1, p2)):
                    m = mm(pt[:], tb["from_virtual"][:, j, :], qx[0:NV, :, :], start=True, stop=True)
                m.then_inc(v_spread, 1)
                pe.wait_ge(v_maps, b + 1)

                def front_turn(n, s):
                    pe.wait_ge(g_done, n + 1)
                    pe.wait_ge(xt_kept, PRIMED + n)
                    turn(g[s]).then_inc(xt_made, 1)

                def front_hilbert(n, s):
                    pe.wait_ge(xt_kept, PRIMED + n + 1)
                    pe.wait_ge(h_kept, PRIMED + n)
                    hilbert().then_inc(h_made, 1)

                def mix(n, s):
                    def mat(j):
                        return bd[s][:, j, :, :].rearrange("p c h -> p (c h)")
                    h_row = hs[s][:, :, 0:HALF]
                    pe.wait_ge(bd_ready, n + 1)
                    pe.wait_ge(t1_done, PRIMED + n)
                    mm(p1[:], mat(2), g[s][:], start=True, stop=False)
                    pe.wait_ge(t2_done, PRIMED + n)
                    mm(p2[:], mat(4), g[s][:], start=True, stop=False)
                    pe.wait_ge(h_kept, PRIMED + n + 1)
                    pe.wait_ge(x1_done, PRIMED + n)
                    edge_terms(mat, hs[s], P)
                    mm(p1[:], mat(3), h_row, start=False, stop=True).then_inc(p1_ready, 1)
                    mm(p2[:], mat(5), h_row, start=False, stop=True).then_inc(p2_ready, 1)
                    mm(p0[:], mat(0), g[s][:], start=True, stop=False)
                    mm(p0[:], mat(1), h_row, start=False, stop=True).then_inc(p0_ready, 1)

                front_turn(b * T, 0)
                front_hilbert(b * T, 0)
                with pe.Fori(0, T // 2 - 1) as i:
                    for s in range(2):
                        n = b * T + i * 2 + s
                        front_turn(n + 1, 1 - s)
                        mix(n, s)
                        front_hilbert(n + 1, 1 - s)
                front_turn(b * T + T - 1, 1)
                mix(b * T + T - 2, 0)
                front_hilbert(b * T + T - 1, 1)
                mix(b * T + T - 1, 1)

                group_stats(b * 2 + 2)

                pe.wait_ge(x1_done, PRIMED + (b + 1) * T)
                for r in range(R + 1):
                    mm(p0[:], tb["ident"][:], img[:, r, :], start=(r == 0), stop=False, skip_group_check=True)
                for r in range(T - R, T):
                    m = mm(p0[:], tb["prev"][:], img[:, r, :], start=False, stop=(r == T - 1), skip_group_check=True)
                m.then_inc(col_summed, 1)

                def move_on(t, came, row_in, left, row_out_):
                    pe.wait_ge(row_padded, b * T + t + 1)
                    mm(p0[:], tb[came][:], img[:, row_in, :], start=False, stop=False, skip_group_check=True)
                    mm(p0[:], tb[left][:], img[:, row_out_, :], start=False, stop=True,
                       skip_group_check=True).then_inc(col_summed, 1)

                with pe.Fori(0, R) as t:
                    move_on(t, "ident", t + (R + 1), "neg_prev", t + (T - R))
                with pe.Fori(R, T - R - 1) as t:
                    move_on(t, "ident", t + (R + 1), "neg_ident", t - R)
                with pe.Fori(T - R - 1, T - 1) as t:
                    move_on(t, "next_", t - (T - R - 1), "neg_ident", t - R)

        @block.scalar
        def _(act):
            def copy(out_, in_):
                return nc.scalar.activation(out_, in_, ACT.Identity)

            def deviation(n):
                act.wait_ge(s_var, n)
                nc.scalar.activation(sc[:, 5:6], sc[:, 4:5], ACT.Sqrt).then_inc(s_sd, 1)

            act.wait_ge(setup_done, 1)
            with act.Fori(0, B) as b:
                deviation(b * 2 + 1)
                act.wait_ge(s_vscale, b + 1)
                act.wait_ge(uv_summed, PRIMED + (b + 1) * (T // 4))
                act.wait_ge(row_out, PRIMED + b * T)
                nc.scalar.activation(halves(g[0])[0:NV], parity(uv_ps[0:NV, :]), ACT.Identity,
                                     bias=sc[0:NV, 13:14], scale=sc[0:NV, 12:13]).then_inc(vg_done, 1)
                act.wait_ge(vxt_made, b + 1)
                copy(xT[:, :, 0:NV], xt_ps[:, :, 0:NV]).then_inc(vxt_kept, 1)
                act.wait_ge(vh_made, b + 1)
                copy(hs[0][0:NV], h_ps[0:NV, :, 0:HALF + NZ]).then_inc(vh_kept, 1)
                act.wait_ge(v_maps, b + 1)

                def normalise(n, t, s):
                    nc.scalar.activation(halves(g[s]), parity(img[:, t, :]), ACT.Identity,
                                         bias=sc[:, 9:10], scale=sc[:, 8:9]).then_inc(g_done, 1)

                def keep_turned(n):
                    act.wait_ge(xt_made, n + 1)
                    copy(xT, xt_ps[:]).then_inc(xt_kept, 1)

                def keep_hilbert(n, s):
                    act.wait_ge(h_made, n + 1)
                    copy(hs[s], h_ps[:, :, 0:HALF + NZ]).then_inc(h_kept, 1)

                normalise(b * T, 0, 0)
                keep_turned(b * T)
                normalise(b * T + 1, 1, 1)
                keep_hilbert(b * T, 0)
                with act.Fori(0, T // 2 - 1) as i:
                    for s in range(2):
                        n = b * T + i * 2 + s
                        keep_turned(n + 1)
                        act.wait_ge(p0_ready, PRIMED + n + 1)
                        normalise(n + 2, i * 2 + (s + 2), s)
                        keep_hilbert(n + 1, 1 - s)
                keep_turned(b * T + T - 1)
                keep_hilbert(b * T + T - 1, 1)

                deviation(b * 2 + 2)
                act.wait_ge(s_scale, b * 2 + 2)
                act.wait_ge(pads_zero, b + 1)

                def pad_row(n, t, s):
                    act.wait_ge(col_summed, n + 1)
                    nc.scalar.activation(padded[s][:, K:K + W], p0[:], ACT.Identity,
                                         bias=box_bias[:, bass.ds(t, 1)],
                                         scale=sc[:, 10:11]).then_inc(row_padded, 1)

                for s in range(2):
                    pad_row(b * T + s, s, s)
                with act.Fori(1, T // 2) as i:
                    for s in range(2):
                        act.wait_ge(row_summed, b * T + i * 2 + (s - 1))
                        pad_row(b * T + i * 2 + s, i * 2 + s, s)

        @block.vector
        def _(dve):
            V = nc.vector
            count = [0]

            def link(ins, s=setup_chain):
                count[0] += 1
                ins.then_inc(s, 1)
                dve.wait_ge(s, count[0])

            V.memset(sc[:], 0.0)
            V.memset(spaced, 0.0).then_inc(zeroed, 1)
            dve.wait_ge(zeroed, 1)
            dve.wait_ge(tab_in, 16 * len(TABLES))
            dve.wait_ge(w_in, 16 * (2 * (HB + 3) + 2))
            wr, wi = raw
            link(V.tensor_copy(aa[:, 0, 0], wr[:, :, 1]))
            link(V.tensor_copy(aa[:, 1, 0], wi[:, :, 1]))
            link(V.tensor_tensor(aa[:, 0, 1], wr[:, :, 0], wr[:, :, 2], ALU.add))
            link(V.tensor_tensor(aa[:, 1, 1], wi[:, :, 0], wi[:, :, 2], ALU.add))
            link(V.tensor_tensor(aa[:, 0, 2], wi[:, :, 0], wi[:, :, 2], ALU.subtract))
            link(V.tensor_tensor(aa[:, 1, 2], wr[:, :, 2], wr[:, :, 0], ALU.subtract))
            ar, ai = aa[:, 0], aa[:, 1]

            def combine(dst, re, im, sr, si):
                def pair(j, a, op, sign):
                    if sign > 0 or op == ALU.subtract:
                        u, v = (0, 2) if sign > 0 else (2, 0)
                        link(V.tensor_tensor(dst(j), a[..., u], a[..., v], op))
                    else:
                        link(V.scalar_tensor_tensor(dst(j), a[..., 0], -1.0, a[..., 2], ALU.mult, ALU.subtract))
                link(V.tensor_scalar(dst(0), re[..., 1], float(sr), None, ALU.mult))
                link(V.tensor_scalar(dst(1), im[..., 1], float(-si), None, ALU.mult))
                pair(2, re, ALU.add, sr)
                pair(3, im, ALU.add, -si)
                pair(4, im, ALU.subtract, si)
                pair(5, re, ALU.subtract, sr)

            combine(lambda j: base[:, :, j], ar, ai, 1, 1)
            for j in range(6):
                def rowwise(f):
                    return base[:, f, j].unsqueeze(1).broadcast_to([P, T, C])

                def trig(f):
                    return tb["trig_h"][:, f].unsqueeze(2).broadcast_to([P, T, C])
                link(V.tensor_tensor(scr, rowwise(1), trig(0), ALU.mult))
                link(V.tensor_tensor(smat[:, :, j], scr, rowwise(0), ALU.add))
                link(V.tensor_tensor(scr, rowwise(2), trig(1), ALU.mult))
                link(V.tensor_tensor(smat[:, :, j], scr, smat[:, :, j], ALU.add))
            for blk, krow, col, swap, sr, si in ((0, 0, 1, False, 1, 1), (0, 0, 2, True, 1, -1),
                                                 (1, 2, 0, False, 1, 1), (2, 2, 0, True, -1, 1)):
                rows = slice(32 * blk, 32 * blk + C)
                re, im = (a[rows, :, krow] for a in (vraw[::-1] if swap else vraw))
                combine(lambda j: spaced[rows, j, col * C:(col + 1) * C], re, im, sr, si)
            V.memset(sc[:, 17:18], 0.0).then_inc(vmat_spaced, 1)
            link(V.tensor_scalar(bias_row[:], hker, bcol[:, 1:2], -1.0, ALU.mult, ALU.mult))
            link(V.tensor_tensor(bias_row[:, 0:1], bias_row[:, 0:1], bcol[:, 0:1], ALU.add))
            for primed in (t1_done, t2_done, x1_done, xt_kept, h_kept, q3_done, p0_ready, qx_done, uv_summed,
                           row_out, *stored):
                dve.sem_inc(primed, PRIMED)
            V.memset(sc[:, 16:17], 0.0).then_inc(setup_done, 1)

            links = [0]

            def statistics(n, b):
                def lk(ins):
                    links[0] += 1
                    ins.then_inc(chain, 1)
                    dve.wait_ge(chain, b * LINKS + links[0])
                V.memset(sc[:, 19:20], 0.0)
                V.bn_aggr(sc[:, 0:2], stat[:].rearrange("p t s -> p (t s)")).then_inc(s_mean, 1)
                dve.wait_ge(s_gmean, n)
                dve.wait_ge(s_mean, n)
                lk(V.tensor_copy(sc[:, 6:7], c_ps[:, 16:17]))
                lk(V.tensor_tensor(sc[:, 2:3], sc[:, 0:1], sc[:, 6:7], ALU.subtract))
                V.scalar_tensor_tensor(sc[:, 3:4], sc[:, 2:3], sc[:, 2:3], sc[:, 1:2],
                                       ALU.mult, ALU.add).then_inc(s_dev, 1)
                dve.wait_ge(s_gvar, n)
                V.tensor_scalar(sc[:, 4:5], c_ps[:, 17:18], EPS, None, ALU.add).then_inc(s_var, 1)
                dve.wait_ge(s_sd, n)
                dve.wait_ge(s_var, n)
                lk(V.reciprocal(sc[:, 7:8], sc[:, 5:6]))
                lk(V.scalar_tensor_tensor(sc[:, 11:12], sc[:, 7:8], sc[:, 7:8], sc[:, 4:5], ALU.mult, ALU.mult))
                lk(V.tensor_scalar(sc[:, 11:12], sc[:, 11:12], -0.5, 1.5, ALU.mult, ALU.add))
                lk(V.tensor_tensor(sc[:, 8:9], sc[:, 7:8], sc[:, 11:12], ALU.mult))
                lk(V.scalar_tensor_tensor(sc[:, 9:10], sc[:, 8:9], -1.0, sc[:, 6:7], ALU.mult, ALU.mult))
                lk(V.tensor_scalar(sc[:, 10:11], sc[:, 8:9], 1.0 / (K * K), None, ALU.mult))
                lk(V.tensor_scalar(sc[:, 14:15], sc[:, 9:10], 1.0 / (K * K), None, ALU.mult))
                V.tensor_scalar(box_bias[:], tb["row_count"][:], sc[:, 14:15], None,
                                ALU.mult).then_inc(s_scale, 1)

            LINKS = 2 * 9 + 3

            with dve.Fori(0, B) as b:
                links[0] = 0

                def lk(ins):
                    links[0] += 1
                    ins.then_inc(chain, 1)
                    dve.wait_ge(chain, b * LINKS + links[0])

                for k in [*range(1, NCH), 0]:
                    with dve.Fori(0, CHUNK) as r:
                        dve.wait_ge(loaded[k], b * 16 + 16)
                        V.bn_stats(stat[:, r + k * CHUNK, :], img[:, r + k * CHUNK, :]).then_inc(rows_counted, 1)
                dve.wait_ge(rows_counted, (b + 1) * T)
                statistics(b * 2 + 1, b)
                dve.wait_ge(s_vsc_ps, b + 1)
                V.tensor_copy(sc[0:NV, 12:13], c_ps[0:NV, 18:19])
                V.memset(sc[:, 13:14], 0.0)
                lk(V.memset(sc[:, 15:16], 0.0))
                V.tensor_copy(sc[0:C, 13:14], c_ps[0:C, 19:20]).then_inc(s_vscale, 1)
                for s in range(2):
                    dve.wait_ge(stored[s], PRIMED + b * (16 * T // 4))
                dve.wait_ge(v_mixed, b + 1)

                def term(dst, pt, cc, wave, rows):
                    for a in range(2):
                        ins = V.scalar_tensor_tensor(dst[0:rows, a, :], pt[0:rows, a * HALF:(a + 1) * HALF],
                                                     c_ps[0:rows, cc + a:cc + a + 1], wave[0:rows, a, :],
                                                     ALU.add, ALU.mult)
                    return ins
                term(t1, p1, 4, cosw, NV)
                lk(term(t2, p2, 0, sinw, NV))
                lk(V.tensor_tensor(t1[0:NV], t1[0:NV], t2[0:NV], ALU.add))
                for a in range(2):
                    ins = V.scalar_tensor_tensor(qx[0:NV, a, :], p0[0:NV, a * HALF:(a + 1) * HALF],
                                                 c_ps[0:NV, 2 + a:3 + a], t1[0:NV, a, :], ALU.add, ALU.add)
                ins.then_inc(v_rows, 1)
                dve.wait_ge(v_spread, b + 1)
                for j, pt in enumerate((p0, p1, p2)):
                    ins = V.tensor_copy(rmap[:, j], halves(pt[:]))
                ins.then_inc(v_maps, 1)
                dve.wait_ge(v_maps, b + 1)
                assert links[0] <= LINKS

                def wrap_rows(n, t, s):
                    V.scalar_tensor_tensor(wadd[s], rmap[:, 1], tb["trig_h"][:, 0, bass.ds(t, 1)], rmap[:, 0],
                                           ALU.mult, ALU.add).then_inc(wa_done, 1)
                    dve.wait_ge(wa_done, n + 1)
                    V.scalar_tensor_tensor(wadd[s], rmap[:, 2], tb["trig_h"][:, 1, bass.ds(t, 1)], wadd[s],
                                           ALU.mult, ALU.add).then_inc(w_done, 1)

                def row(n, t, s, last=False):
                    dve.wait_ge(p1_ready, n + 1)
                    dve.wait_ge(q3_done, PRIMED + n)
                    term(t1, p1, 4, cosw, P).then_inc(t1_done, 1)
                    dve.wait_ge(p2_ready, n + 1)
                    term(t2, p2, 0, sinw, P).then_inc(t2_done, 1)
                    if not last:
                        wrap_rows(n + 1, t + 1, 1 - s)
                    dve.wait_ge(p0_ready, PRIMED + n + 1)
                    dve.wait_ge(q3_done, PRIMED + n + 1)
                    for a in range(2):
                        ins = V.scalar_tensor_tensor(parity(img[:, t, :])[:, a, :], p0[:, a * HALF:(a + 1) * HALF],
                                                     c_ps[:, 2 + a:3 + a], qx[:, a, :], ALU.add, ALU.add)
                    ins.then_inc(x1_done, 1)
                    dve.wait_ge(x1_done, PRIMED + n + 1)
                    V.bn_stats(stat[:, t, :], img[:, t, :]).then_inc(x1_counted, 1)

                dve.wait_ge(qx_done, PRIMED + b * T)
                wrap_rows(b * T, 0, 0)
                dve.wait_ge(g_done, b * T + 1)
                V.tensor_tensor(img[:, 0, :], img[:, 0, :], bias_row[:], ALU.add).then_inc(bias_added, 1)
                with dve.Fori(0, T // 2 - 1) as i:
                    for s in range(2):
                        row(b * T + i * 2 + s, i * 2 + s, s)
                row(b * T + T - 2, T - 2, 0)
                row(b * T + T - 1, T - 1, 1, last=True)
                dve.wait_ge(x1_counted, (b + 1) * T)
                statistics(b * 2 + 2, b)
                assert links[0] == LINKS, links[0]
                for s in range(2):
                    V.memset(padded[s][:, 0:K], 0.0)
                    ins = V.memset(padded[s][:, K + W:PADW], 0.0)
                ins.then_inc(pads_zero, 1)
                dve.wait_ge(pads_zero, b + 1)

                def run_sum(n, s):
                    dve.wait_ge(row_padded, n + 1)
                    V.tensor_tensor_scan(sums[s], padded[s][:, K:K + SUMW], padded[s][:, 0:SUMW], 0.0,
                                         ALU.add, ALU.subtract).then_inc(row_summed, 1)

                for s in range(2):
                    run_sum(b * T + s, s)
                with dve.Fori(1, T // 2) as i:
                    for s in range(2):
                        dve.wait_ge(row_out, PRIMED + b * T + i * 2 + (s - 1))
                        run_sum(b * T + i * 2 + s, s)

        @block.gpsimd
        def _(pool):
            G = nc.gpsimd
            pool.wait_ge(setup_done, 1)
            pool.wait_ge(tab_in, 16 * len(TABLES))
            with pool.Fori(0, B) as b:
                for q, k in enumerate([*range(1, NCH), 0]):
                    for s in range(2):
                        if q:
                            pool.wait_ge(uv_summed, PRIMED + b * (T // 4) + (2 * q + s - 1))
                        elif s == 0:
                            pool.wait_ge(uv_summed, PRIMED + b * (T // 4))
                        rows = tb["virt_h"][:, k * CHUNK + 4 * s:k * CHUNK + 4 * s + 4, :].rearrange("p t j -> p (t j)")
                        G.tensor_tensor(uvw[s][:, :, 0:C], rows.unsqueeze(2).broadcast_to([P, 12, C]),
                                        tb["c_mask"][:].unsqueeze(1).broadcast_to([P, 12, C]),
                                        ALU.mult).then_inc(uvw_ready, 1)

                def spread(t, s):
                    G.tensor_tensor(bd[s][:], smat[:, t, :, :].unsqueeze(3).broadcast_to([P, 6, C, HB]),
                                    tb["hb_mask"][:].unsqueeze(1).unsqueeze(1).broadcast_to([P, 6, C, HB]),
                                    ALU.mult).then_inc(bd_ready, 1)

                def row(n, t, s, last=False):
                    if not last:
                        pool.wait_ge(p0_ready, PRIMED + n)
                        spread(t + 1, 1 - s)
                    pool.wait_ge(w_done, n + 1)
                    pool.wait_ge(x1_done, PRIMED + n)
                    G.tensor_tensor(qx[:], wadd[s], parity(img[:, t, :]), ALU.add).then_inc(qx_done, 1)
                    pool.wait_ge(t2_done, PRIMED + n + 1)
                    G.tensor_tensor(t1, t1, t2, ALU.add).then_inc(q_done, 1)
                    pool.wait_ge(q_done, n + 1)
                    pool.wait_ge(qx_done, PRIMED + n + 1)
                    G.tensor_tensor(qx[:], qx[:], t1, ALU.add).then_inc(q3_done, 1)

                pool.wait_ge(p0_ready, PRIMED + b * T)
                pool.wait_ge(bias_added, b + 1)
                spread(0, 0)
                with pool.Fori(0, T // 2 - 1) as i:
                    for s in range(2):
                        row(b * T + i * 2 + s, i * 2 + s, s)
                row(b * T + T - 2, T - 2, 0)
                row(b * T + T - 1, T - 1, 1, last=True)

                with pool.Fori(0, T // 4) as i:
                    for s in range(2):
                        pool.wait_ge(stored[s], PRIMED + (b * (T // 4) + i) * 16)
                        for r in range(2):
                            n = b * T + i * 4 + (2 * s + r)
                            pool.wait_ge(row_summed, n + 1)
                            G.tensor_tensor(ob[s][:, r, :], sums[r][:, R:R + W], img[:, i * 4 + (2 * s + r), :],
                                            ALU.add).then_inc(row_out, 1)


_INS = ["x", "L0_conv_w_real", "L0_conv_w_imag", "L0_conv_b_real", "L0_conv_b_imag"]


def kernel(**inputs):
    import concourse.bacc as bacc
    from concourse.bass_utils import run_bass_kernel_spmd

    nc = bacc.Bacc("TRN2", target_bir_lowering=False, num_devices=1)
    arrays, args = {}, []
    for name in _INS:
        a = np.ascontiguousarray(inputs[name])
        arrays[f"in_{name}"] = a
        args.append(nc.dram_tensor(f"in_{name}", a.shape, mybir.dt.from_np(a.dtype), kind="ExternalInput").ap())
    tab = {}
    for name, a in tables().items():
        arrays[f"tab_{name}"] = a
        tab[name] = nc.dram_tensor(f"tab_{name}", a.shape, mybir.dt.from_np(a.dtype), kind="ExternalInput").ap()
    out = nc.dram_tensor("out_0", (B, C, H, W), F32, kind="ExternalOutput").ap()
    build(nc, *args, tab, out)
    r = run_bass_kernel_spmd(nc, [arrays], core_ids=[0])
    return r.results[0]["out_0"]
```

```python
from contextlib import ExitStack

import numpy as np

import concourse.bass as bass
from concourse import mybir

F32 = mybir.dt.float32
F16 = mybir.dt.float16
ALU = mybir.AluOpType
ACT = mybir.ActivationFunctionType

P = 128
B, C, H, W = 8, 16, 512, 512
HB = P // C
T = H // HB
GROUP = 2 * HB
HALF = W // 2
NZ = 5
HZ = HALF + 8
K = 15
R = K // 2
EPS = 1e-5
CHUNK = 8
NCH = T // CHUNK
PADW = K + W + R
SUMW = W + R
NDIFF = T - K
AHEAD = NCH // 2
PRIMED = 1
ROW_SCALE = 32.0
MAT_SCALE = 2048.0
TAB_SCALE = 65536.0
NS = 4
NV = 3 * C
QUARTER = HALF // 4

TABLES = ["ident", "prev", "next_", "neg_ident", "neg_prev", "group_mean", "cosw",
          "to_virtual", "from_virtual", "c_mask", "trig_h", "virt_h", "row_count", "hilbert_kernel",
          "ident16", "hb_mask16", "hilbert16"]


def tables():
    th = 2 * np.pi / W
    p = np.arange(P)
    hb, c = p // C, p % C
    h = (hb[:, None] * T + np.arange(T)[None, :])
    eye = np.eye(P)
    prev = np.zeros((P, P))
    nxt = np.zeros((P, P))
    for m in range(P):
        if hb[m] != 0:
            prev[m - C, m] = 1
        if hb[m] != HB - 1:
            nxt[m + C, m] = 1

    def kern(n):
        n = np.asarray(n)
        odd = n % 2 == 1
        return np.where(odd, 2.0 / W / np.tan(np.pi * np.where(odd, n, 1) / W), 0.0)

    def split(v):
        high = v.astype(np.float16)
        return np.stack([high, (v - high).astype(np.float16)], 1)

    hil = np.zeros((P, 4, HALF + NZ))
    for k in range(4):
        par, half = k // 2, k % 2
        w = 2 * (P * half + np.arange(P)) + par
        wo = 2 * np.arange(HALF) + (1 - par)
        hil[:, k, :HALF] = kern(wo[None, :] - w[:, None])
        hil[:, k, HALF + 0] = 2.0 / W
        hil[:, k, HALF + 1] = np.sin(th * w) / W
        hil[:, k, HALF + 2] = -np.cos(th * w) / W
        hil[:, k, HALF + 3] = -2.0 / W
        hil[:, k, HALF + 4] = -np.sin(th * w) / W
    wsep = np.stack([2 * np.arange(-QUARTER, HALF), 2 * np.arange(-QUARTER, HALF) + 1])
    tov = np.zeros((P, NV))
    fromv = np.zeros((NV, 3, P))
    for cc in range(C):
        for j in range(3):
            tov[cc, j * C + cc] = 1
            fromv[j * C + cc, j, cc::C] = -1
    trig = np.stack([np.cos(th * h), np.sin(th * h)], 1)
    virt = np.stack([np.ones_like(h) / H, np.cos(th * h) / H, np.sin(th * h) / H], 2)
    count = np.minimum(h + R, H - 1) - np.maximum(h - R, 0) + 1
    count = count[:, [*range(R + 1), *range(T - R - 1, T)]]
    out = {
        "ident": eye, "prev": prev, "next_": nxt, "neg_ident": -eye, "neg_prev": -prev,
        "group_mean": (c[:, None] // 2 == c[None, :] // 2) / GROUP,
        "hilbert16": split(hil * TAB_SCALE),
        "cosw": np.broadcast_to(np.cos(th * wsep), (P, *wsep.shape)),
        "to_virtual": tov, "from_virtual": fromv,
        "ident16": eye,
        "hb_mask16": np.broadcast_to((hb[:, None] == np.arange(HB)[None, :])[:, :, None], (P, HB, C)),
        "c_mask": c[:, None] == np.arange(C)[None, :],
        "trig_h": trig, "virt_h": virt, "row_count": count,
        "hilbert_kernel": np.tile(kern(np.arange(W)), (P, 1)),
    }
    return {k: np.ascontiguousarray(v, dtype=np.float16 if k.endswith("16") else np.float32)
            for k, v in out.items()}


def build(nc, x, w_real, w_imag, b_real, b_imag, tab, out):
    x_v = x.rearrange("b c (hb t) w -> b hb c (t w)", hb=HB)
    out_v = out.rearrange("b c (hb t) w -> b hb c (t w)", hb=HB)
    with ExitStack() as ctx:
        def sb(name, shape, dt=F32):
            return ctx.enter_context(nc.sbuf_tensor(name, shape, dt))

        def sem(name):
            return ctx.enter_context(nc.semaphore(name))

        img = sb("img", [P, T, W])
        smat = sb("smat", [P, T, 12, C], F16)
        tb = {n: sb(n, list(tab[n].shape), tab[n].dtype) for n in TABLES if n != "hilbert_kernel"}
        vmat = sb("vmat", [NV, 12, NV], F16)
        uvw = [sb(f"uvw{s}", [P, 4 * 3, C]) for s in range(2)]
        rmap = sb("rmap", [P, 3, 2, HALF])
        bias_row = sb("bias_row", [P, W])
        cosw, sinw = tb["cosw"][:, :, QUARTER:], tb["cosw"][:, :, 0:HALF]
        sizes = [W, W, W, W, 2 * HZ, 2 * HZ]
        work = sb("work", [P, sum(sizes)])
        at = np.cumsum([0] + sizes)
        piece = [work[:, int(at[i]):int(at[i + 1])] for i in range(len(sizes))]
        g32 = piece[0]
        gp = [piece[1 + s].bitcast(F16).rearrange("p (l j) -> p l j", l=2) for s in range(2)]
        xT = piece[3].bitcast(F16).rearrange("p (k m) -> p k m", k=8)
        hp = [piece[4 + s].bitcast(F16).rearrange("p (l a n) -> p l a n", l=2, a=2) for s in range(2)]
        padded = [work[:, s * PADW:(s + 1) * PADW] for s in range(2)]
        sums = [work[:, 2 * PADW + s * SUMW:2 * PADW + (s + 1) * SUMW] for s in range(2)]
        assert 2 * (PADW + SUMW) <= sum(sizes)
        ob = [sb(f"ob{s}", [P, 2, W]) for s in range(2)]
        t1, t2 = (ob[0][:, i, :].rearrange("p (a j) -> p a j", a=2) for i in range(2))
        wadd = [ob[1][:, i, :].rearrange("p (a j) -> p a j", a=2) for i in range(2)]
        more = sb("more", [P, 4 * W])
        ob += [more[:, i * 2 * W:(i + 1) * 2 * W].rearrange("p (r w) -> p r w", r=2) for i in range(2)]
        bd = [more[:, s * 6 * P:(s + 1) * 6 * P].bitcast(F16).rearrange("p (j h c) -> p j h c", j=12, h=HB)
              for s in range(2)]
        qx = more[:, 12 * P:16 * P].rearrange("p (a j) -> p a j", a=2)
        base0 = sb("base0", [P, 2, HALF])
        edge = sb("edge", [P, 8])
        diff = [rmap[:, s] .rearrange("p a j -> p (a j)") for s in range(2)]
        stat = sb("stat", [P, T, 6])
        sc = sb("sc", [P, 24])
        box_bias = sb("box_bias", [P, 2 * (R + 1)])

        xt_ps = ctx.enter_context(nc.psum_tensor("xt_ps", [P, 8, P], F16))
        h_ps = ctx.enter_context(nc.psum_tensor("h_ps", [P, 2, W], F32))
        p0 = ctx.enter_context(nc.psum_tensor("p0", [P, W], F32))
        p1 = ctx.enter_context(nc.psum_tensor("p1", [P, W], F32))
        p2 = ctx.enter_context(nc.psum_tensor("p2", [P, W], F32))
        c_ps = ctx.enter_context(nc.psum_tensor("c_ps", [P, W], F32))
        uv_ps = ctx.enter_context(nc.psum_tensor("uv_ps", [P, W], F32))

        tab_in, w_in, zeroed = sem("tab_in"), sem("w_in"), sem("zeroed")
        setup_chain, setup_done = sem("setup_chain"), sem("setup_done")
        vmat_spaced, vmat_in = sem("vmat_spaced"), sem("vmat_in")
        loaded = [sem(f"loaded{k}") for k in range(NCH)]
        uvw_ready, uv_summed, rows_counted = sem("uvw_ready"), sem("uv_summed"), sem("rows_counted")
        chain = sem("chain")
        s_mean, s_gmean, s_dev, s_gvar = sem("s_mean"), sem("s_gmean"), sem("s_dev"), sem("s_gvar")
        s_var, s_sd, s_scale, s_vsc_ps, s_vscale = (sem("s_var"), sem("s_sd"), sem("s_scale"),
                                                    sem("s_vsc_ps"), sem("s_vscale"))
        vg_done, vxt_made, vxt_kept, vh_made, vh_kept = (sem("vg_done"), sem("vxt_made"), sem("vxt_kept"),
                                                         sem("vh_made"), sem("vh_kept"))
        v_mixed, v_rows, v_spread, v_maps = sem("v_mixed"), sem("v_rows"), sem("v_spread"), sem("v_maps")
        g_done, xt_made, xt_kept, h_made, h_kept = (sem("g_done"), sem("xt_made"), sem("xt_kept"),
                                                    sem("h_made"), sem("h_kept"))
        bd_ready, p1_ready, p2_ready, p0_ready = sem("bd_ready"), sem("p1_ready"), sem("p2_ready"), sem("p0_ready")
        t1_done, t2_done, q_done, q3_done = sem("t1_done"), sem("t2_done"), sem("q_done"), sem("q3_done")
        wa_done, w_done, qx_done, x1_done = sem("wa_done"), sem("w_done"), sem("qx_done"), sem("x1_done")
        bias_added, x1_counted = sem("bias_added"), sem("x1_counted")
        moved = sem("moved")
        vg_split, vh_split, g_split, h_split = sem("vg_split"), sem("vh_split"), sem("g_split"), sem("h_split")
        g_used, edge_ready, edge_kept, base_done = sem("g_used"), sem("edge_ready"), sem("edge_kept"), sem("base_done")
        max_w, max_all = sem("max_w"), sem("max_all")
        pads_zero, row_summed, row_out = sem("pads_zero"), sem("row_summed"), sem("row_out")
        col_summed = [sem(f"col_summed{a}") for a in range(2)]
        row_padded = [sem(f"row_padded{a}") for a in range(2)]
        stored = [sem(f"stored{s}") for s in range(NS)]

        flat = img[:, 0:24, :].rearrange("p t w -> p (t w)")
        raw = [flat[:, i * 144:(i + 1) * 144].rearrange("p (o a b) -> p o a b", o=C, a=3) for i in range(2)]
        vraw = [flat[:, (2 + i) * 144:(3 + i) * 144].rearrange("p (o a b) -> p o a b", o=C, a=3)
                for i in range(2)]
        aa = flat[:, 1024:1024 + 288].rearrange("p (r f o b) -> p r f o b", r=2, f=3, o=C)
        base = flat[:, 1536:1536 + 288].rearrange("p (f j o) -> p f j o", f=3, j=6)
        hker = flat[:, 2048:2048 + W]
        scr = flat[:, 4096:4096 + T * C].rearrange("p (t o) -> p t o", o=C)
        sfull = flat[:, 5120:5120 + T * C].rearrange("p (t o) -> p t o", o=C)
        spaced = flat[:, 8192:8192 + 6 * NV].rearrange("p (j m) -> p j m", j=6)
        spaced16 = flat[:, 9216:9216 + 6 * NV].bitcast(F16).rearrange("p (j m) -> p j m", j=12)
        unscale = sc[:, 22:23]
        bcol = sc[:, 20:22]

        def parity(ap):
            return ap.rearrange("p (j two) -> p two j", two=2)

        def halves(ap):
            return ap.rearrange("p (a j) -> p a j", a=2)

        block = ctx.enter_context(nc.Block())

        @block.sync
        def _(sp):
            for n in TABLES:
                dst = hker if n == "hilbert_kernel" else tb[n][:]
                sp.dma_start(dst, tab[n]).then_inc(tab_in, 16)
            sp.wait_ge(zeroed, 1)
            for i, wr in enumerate((w_real, w_imag)):
                w_flat = wr.rearrange("i o a b -> i (o a b)")
                for k in range(HB):
                    sp.dma_start(flat[k * C:(k + 1) * C, i * 144:(i + 1) * 144], w_flat).then_inc(w_in, 16)
                for k in range(3):
                    sp.dma_start(flat[32 * k:32 * k + C, (2 + i) * 144:(3 + i) * 144], w_flat).then_inc(w_in, 16)
            for i, br in enumerate((b_real, b_imag)):
                sp.dma_start(sc[0:C, 20 + i:21 + i], br.rearrange("(c o) -> c o", o=1)).then_inc(w_in, 16)

            def load(b, k):
                sp.dma_start(img[:, k * CHUNK:(k + 1) * CHUNK, :].rearrange("p t w -> p (t w)"),
                             x_v[b, :, :, k * CHUNK * W:(k + 1) * CHUNK * W]).then_inc(loaded[k], 16)

            def store(b, j, s):
                sp.wait_ge(row_out, PRIMED + b * T + j * 2 + 2)
                sp.dma_start(out_v[b, :, :, bass.ds(j * (2 * W), 2 * W)],
                             ob[s][:].rearrange("p t w -> p (t w)")).then_inc(stored[s], 16)

            sp.wait_ge(vmat_spaced, 1)
            for k in range(3):
                sp.dma_start(vmat[k * C:(k + 1) * C, :, :].rearrange("p j m -> p (j m)"),
                             spaced16[32 * k:32 * k + C, :, :].rearrange("p j m -> p (j m)")).then_inc(vmat_in, 16)
            sp.wait_ge(vmat_in, 48)
            sp.wait_ge(setup_done, 1)
            for k in [*range(1, NCH), 0]:
                load(0, k)

            with sp.Fori(0, B - 1) as b:
                for j in range(8):
                    store(b, j, j % NS)
                for k in range(1, NCH - 1):
                    for j in range(4 * k + 4, 4 * k + 8):
                        store(b, j, j % NS)
                    sp.wait_ge(col_summed[1], b * T + CHUNK * (k + 1) + R + 1)
                    load(b + 1, k)
                for k in (NCH - 1, 0):
                    load(b + 1, k)
            with sp.Fori(0, T // (2 * NS)) as i:
                for s in range(NS):
                    store(B - 1, i * NS + s, s)
            for s in range(NS):
                sp.wait_ge(stored[s], PRIMED + 16 * B * T // (2 * NS))

        @block.tensor
        def _(pe):
            mm = nc.tensor.matmul
            pe.wait_ge(tab_in, 16 * len(TABLES))
            pe.wait_ge(setup_done, 1)
            pe.wait_ge(vmat_in, 48)

            def group_stats(n):
                pe.wait_ge(s_mean, n)
                mm(c_ps[:, 16:17], tb["group_mean"][:], sc[:, 0:1], start=True, stop=True).then_inc(s_gmean, 1)
                pe.wait_ge(s_dev, n)
                mm(c_ps[:, 17:18], tb["group_mean"][:], sc[:, 3:4], start=True, stop=True).then_inc(s_gvar, 1)

            def hold():
                nc.tensor.transpose(xt_ps[:, 0, :], tb["ident16"][:], tb["ident16"][:])

            def turn(parts, rows=P):
                for l in range(2):
                    for k in range(4):
                        m = nc.tensor.transpose(xt_ps[:, 4 * l + k, 0:rows], parts[0:rows, l, k * P:(k + 1) * P],
                                                tb["ident16"][0:rows, 0:rows])
                return m

            def hilbert(rows=P):
                for a in range(2):
                    for half in range(2):
                        k = 2 * (1 - a) + half
                        for i, (lx, lt) in enumerate(((0, 0), (0, 1), (1, 0))):
                            m = mm(h_ps[0:rows, a, 0:HALF + NZ], xT[:, 4 * lx + k, 0:rows],
                                   tb["hilbert16"][:, lt, k, :], start=(half == 0 and i == 0),
                                   stop=(half == 1 and i == 2))
                return m

            def product(dst, mat, j, parts, start, stop):
                for i, (lm, lp) in enumerate(((0, 0), (0, 1), (1, 0))):
                    m = mm(dst, mat(6 * lm + j), parts(lp), start=start and i == 0, stop=stop and i == 2)
                return m

            def edge_terms(mat, hrow, rows):
                def add(c0, c1, j, z, first, last):
                    for i, (lm, lp) in enumerate(((0, 0), (0, 1), (1, 0))):
                        m = mm(c_ps[0:rows, c0:c1], mat(6 * lm + j), z(lp), start=first and i == 0,
                               stop=last and i == 2, skip_group_check=True)
                    return m
                row = hrow[0:rows]

                def opp(f):
                    return lambda l: row[:, l, :, HALF + f:HALF + f + 2].rearrange("p a f -> p f a")

                def same(f):
                    return lambda l: row[:, l, ::-1, HALF + f:HALF + f + 1]
                add(0, 4, 3, opp(0), True, False)
                add(2, 6, 5, opp(2), False, False)
                add(2, 4, 2, same(2), False, False)
                return add(2, 4, 4, same(4), False, True)

            def sum_rows(b, q, k, r):
                s = r // 4
                if r == 0:
                    pe.wait_ge(loaded[k], b * 16 + 16)
                if r % 4 == 0:
                    pe.wait_ge(uvw_ready, b * (T // 4) + (2 * q + s + 1))
                w = uvw[s][:, 3 * (r % 4):3 * (r % 4) + 3, :].rearrange("p j c -> p (j c)")
                m = mm(uv_ps[0:NV, :], w, img[:, k * CHUNK + r, :], start=(q == 0 and r == 0),
                       stop=(q == NCH - 1 and r == CHUNK - 1))
                if r % 4 == 3:
                    m.then_inc(uv_summed, 1)

            def layer0(b):
                group_stats(b * 2 + 1)
                pe.wait_ge(s_scale, b * 2 + 1)
                mm(c_ps[0:NV, 18:20], tb["to_virtual"][:], sc[:, 8:10], start=True, stop=True).then_inc(s_vsc_ps, 1)

                def vm(j):
                    return vmat[:, j, :]
                pe.wait_ge(vg_done, b + 1)
                hold()
                pe.wait_ge(vg_split, b + 1)
                hold()
                turn(gp[0], NV).then_inc(vxt_made, 1)
                pe.wait_ge(vxt_kept, b + 1)
                hilbert(NV).then_inc(vh_made, 1)
                pe.wait_ge(s_vscale, b + 1)
                hold()
                pe.wait_ge(vh_split, b + 1)
                hold()
                edge_terms(vm, hp[0], NV)
                for pt, jg, jh in ((p1, 2, 3), (p2, 4, 5), (p0, 0, 1)):
                    product(pt[0:NV, :], vm, jg, lambda l: gp[0][0:NV, l, :], True, False)
                    m = product(pt[0:NV, :], vm, jh, lambda l: hp[0][0:NV, l, :, 0:HALF], False, True)
                m.then_inc(v_mixed, 1)
                pe.wait_ge(v_rows, b + 1)
                for j, pt in enumerate((p0, p1, p2)):
                    m = mm(pt[:], tb["from_virtual"][:, j, :], qx[0:NV, :, :], start=True, stop=True)
                m.then_inc(v_spread, 1)
                pe.wait_ge(v_maps, b + 1)

                def front_turn(n, s):
                    pe.wait_ge(g_split, n + 1)
                    pe.wait_ge(xt_kept, PRIMED + n)
                    turn(gp[s]).then_inc(xt_made, 1)

                def front_hilbert(n, s):
                    pe.wait_ge(xt_kept, PRIMED + n + 1)
                    pe.wait_ge(h_split, PRIMED + n)
                    hilbert().then_inc(h_made, 1)

                def mix(n, s):
                    def mat(j):
                        return bd[s][:, j].rearrange("p h c -> p (h c)")

                    def g_row(l):
                        return gp[s][:, l, :]

                    def h_row(l):
                        return hp[s][:, l, :, 0:HALF]
                    pe.wait_ge(bd_ready, n + 1)
                    pe.wait_ge(t1_done, PRIMED + n)
                    product(p1[:], mat, 2, g_row, True, False)
                    pe.wait_ge(t2_done, PRIMED + n)
                    product(p2[:], mat, 4, g_row, True, False)
                    pe.wait_ge(base_done, PRIMED + n)
                    product(p0[:], mat, 0, g_row, True, False).then_inc(g_used, 1)
                    pe.wait_ge(h_split, PRIMED + n + 1)
                    pe.wait_ge(edge_kept, PRIMED + n)
                    edge_terms(mat, hp[s], P).then_inc(edge_ready, 1)
                    product(p1[:], mat, 3, h_row, False, True).then_inc(p1_ready, 1)
                    product(p2[:], mat, 5, h_row, False, True).then_inc(p2_ready, 1)
                    product(p0[:], mat, 1, h_row, False, True).then_inc(p0_ready, 1)

                front_turn(b * T, 0)
                front_hilbert(b * T, 0)
                with pe.Fori(0, T // 2 - 1) as i:
                    for s in range(2):
                        n = b * T + i * 2 + s
                        front_turn(n + 1, 1 - s)
                        mix(n, s)
                        front_hilbert(n + 1, 1 - s)
                front_turn(b * T + T - 1, 1)
                mix(b * T + T - 2, 0)
                front_hilbert(b * T + T - 1, 1)
                mix(b * T + T - 1, 1)

                group_stats(b * 2 + 2)

            def layer1(b, follow):
                pe.wait_ge(x1_done, PRIMED + (b + 1) * T)
                for a, bank in enumerate((p0, p1)):
                    for r in range(R + 1):
                        mm(bank[:, 0:HALF], tb["ident"][:], img[:, r, a * HALF:(a + 1) * HALF],
                           start=(r == 0), stop=False, skip_group_check=True)
                    for r in range(T - R, T):
                        m = mm(bank[:, 0:HALF], tb["prev"][:], img[:, r, a * HALF:(a + 1) * HALF],
                               start=False, stop=(r == T - 1), skip_group_check=True)
                    m.then_inc(col_summed[a], 1)

                def move_on(t, *parts):
                    for a, bank in enumerate((p0, p1)):
                        pe.wait_ge(row_padded[a], b * T + t + 1)
                        for i, (mat, row) in enumerate(parts):
                            m = mm(bank[:, 0:HALF], tb[mat][:], row(a), start=False,
                                   stop=(i == len(parts) - 1), skip_group_check=True)
                        m.then_inc(col_summed[a], 1)

                def img_row(t):
                    return lambda a: img[:, t, a * HALF:(a + 1) * HALF]

                def move_diff(t, s):
                    pe.wait_ge(moved, b * NDIFF + t - R + 1)
                    move_on(t, ("ident", lambda a: diff[s][:, a * HALF:(a + 1) * HALF]))

                with pe.Fori(0, R) as t:
                    move_on(t, ("ident", img_row(t + (R + 1))), ("neg_prev", img_row(t + (T - R))))
                move_diff(R, 1)
                with pe.Fori(R // 2 + 1, T // 4) as i:
                    for s in range(2):
                        move_diff(i * 2 + s, s)
                for q in range(AHEAD):
                    for r in range(CHUNK):
                        t = T - CHUNK * (AHEAD - q) + r
                        if t < T - R - 1:
                            move_diff(t, t % 2)
                        elif t < T - 1:
                            move_on(t, ("next_", img_row(t - (T - R - 1))), ("neg_ident", img_row(t - R)))
                        if follow:
                            sum_rows(b + 1, q, q + 1, r)
                if follow:
                    for q in range(AHEAD, NCH):
                        for r in range(CHUNK):
                            sum_rows(b + 1, q, (q + 1) % NCH, r)

            for q in range(NCH):
                for r in range(CHUNK):
                    sum_rows(0, q, (q + 1) % NCH, r)
            with pe.Fori(0, B - 1) as b:
                layer0(b)
                layer1(b, True)
            layer0(B - 1)
            layer1(B - 1, False)

        @block.scalar
        def _(act):
            def copy(out_, in_):
                return nc.scalar.activation(out_, in_, ACT.Identity)

            def high_hilbert(s, rows=P):
                return nc.scalar.activation(hp[s][0:rows, 0, :, 0:HALF + NZ], h_ps[0:rows, :, 0:HALF + NZ],
                                            ACT.Identity, scale=1.0 / TAB_SCALE)

            def deviation(n):
                act.wait_ge(s_var, n)
                nc.scalar.activation(sc[:, 5:6], sc[:, 4:5], ACT.Sqrt).then_inc(s_sd, 1)

            act.wait_ge(setup_done, 1)
            with act.Fori(0, B) as b:
                deviation(b * 2 + 1)
                act.wait_ge(s_vscale, b + 1)
                act.wait_ge(uv_summed, PRIMED + (b + 1) * (T // 4))
                act.wait_ge(row_out, PRIMED + b * T)
                for dst in (gp[0][0:NV, 0, :], g32[0:NV]):
                    ins = nc.scalar.activation(halves(dst), parity(uv_ps[0:NV, :]), ACT.Identity,
                                               bias=sc[0:NV, 13:14], scale=sc[0:NV, 12:13])
                ins.then_inc(vg_done, 1)
                act.wait_ge(vxt_made, b + 1)
                copy(xT[:, :, 0:NV], xt_ps[:, :, 0:NV]).then_inc(vxt_kept, 1)
                act.wait_ge(vh_made, b + 1)
                high_hilbert(0, NV).then_inc(vh_kept, 1)
                act.wait_ge(v_maps, b + 1)

                def normalise(n, t, s):
                    act.wait_ge(g_split, n)
                    nc.scalar.activation(halves(gp[s][:, 0, :]), parity(img[:, t, :]), ACT.Identity,
                                         bias=sc[:, 9:10], scale=sc[:, 8:9])
                    nc.scalar.activation(halves(g32), parity(img[:, t, :]), ACT.Identity,
                                         bias=sc[:, 9:10], scale=sc[:, 8:9]).then_inc(g_done, 1)

                def keep_turned(n):
                    act.wait_ge(xt_made, n + 1)
                    copy(xT, xt_ps[:]).then_inc(xt_kept, 1)

                def keep_hilbert(n, s):
                    act.wait_ge(h_made, n + 1)
                    high_hilbert(s).then_inc(h_kept, 1)

                def keep_base(n):
                    act.wait_ge(p0_ready, PRIMED + n + 1)
                    act.wait_ge(edge_kept, PRIMED + n + 1)
                    act.wait_ge(x1_done, PRIMED + n)
                    for a in range(2):
                        ins = nc.scalar.activation(base0[:, a, :], p0[:, a * HALF:(a + 1) * HALF], ACT.Identity,
                                                   bias=edge[:, 6 + a:7 + a], scale=unscale)
                    ins.then_inc(base_done, 1)

                nc.scalar.activation(halves(gp[0][:, 0, :]), parity(img[:, 0, :]), ACT.Identity,
                                     bias=sc[:, 9:10], scale=sc[:, 8:9])
                nc.scalar.activation(halves(g32), parity(img[:, 0, :]), ACT.Identity,
                                     bias=sc[:, 9:10], scale=sc[:, 8:9]).then_inc(g_done, 1)
                normalise(b * T + 1, 1, 1)
                keep_turned(b * T)
                keep_hilbert(b * T, 0)
                with act.Fori(0, T // 2 - 1) as i:
                    for s in range(2):
                        n = b * T + i * 2 + s
                        keep_turned(n + 1)
                        act.wait_ge(g_used, n + 1)
                        normalise(n + 2, i * 2 + (s + 2), s)
                        keep_base(n)
                        keep_hilbert(n + 1, 1 - s)
                keep_turned(b * T + T - 1)
                keep_base(b * T + T - 2)
                keep_hilbert(b * T + T - 1, 1)
                keep_base(b * T + T - 1)

                deviation(b * 2 + 2)
                act.wait_ge(s_scale, b * 2 + 2)
                act.wait_ge(pads_zero, b + 1)

                def pad_row(t, s, bias_row):
                    if not isinstance(t, int) or t >= 2:
                        act.wait_ge(row_summed, b * T + t - 1)
                    for a, bank in enumerate((p0, p1)):
                        act.wait_ge(col_summed[a], b * T + t + 1)
                        nc.scalar.activation(padded[s][:, K + a * HALF:K + (a + 1) * HALF], bank[:, 0:HALF],
                                             ACT.Identity, bias=box_bias[:, bias_row:bias_row + 1],
                                             scale=sc[:, 10:11]).then_inc(row_padded[a], 1)

                for t in range(R + 1):
                    pad_row(t, t % 2, t)
                with act.Fori((R + 1) // 2, (T - R - 1) // 2) as i:
                    for s in range(2):
                        pad_row(i * 2 + s, s, R)
                for t in range(T - R - 1, T):
                    pad_row(t, t % 2, t - (T - 2 * (R + 1)))

        @block.vector
        def _(dve):
            V = nc.vector
            count = [0]

            def link(ins, s=setup_chain):
                count[0] += 1
                ins.then_inc(s, 1)
                dve.wait_ge(s, count[0])

            V.memset(sc[:], 0.0)
            V.memset(flat[:, 0:4 * 144], 0.0)
            V.memset(spaced, 0.0).then_inc(zeroed, 1)
            dve.wait_ge(zeroed, 1)
            dve.wait_ge(tab_in, 16 * len(TABLES))
            dve.wait_ge(w_in, 16 * (2 * (HB + 3) + 2))
            V.tensor_reduce(sc[:, 0:1], flat[:, 0:2 * 144], mybir.AxisListType.X, ALU.max,
                            apply_absolute_value=True).then_inc(max_w, 1)
            dve.wait_ge(max_all, 1)
            link(V.tensor_scalar(sc[:, 2:3], sc[:, 1:2], 1e-30, None, ALU.max))
            link(V.tensor_scalar(unscale, sc[:, 2:3], 1.0 / (MAT_SCALE * ROW_SCALE), None, ALU.mult))
            link(V.reciprocal(sc[:, 3:4], sc[:, 2:3]))
            link(V.tensor_scalar(flat[:, 0:4 * 144], flat[:, 0:4 * 144], sc[:, 3:4], MAT_SCALE, ALU.mult, ALU.mult))
            link(V.tensor_scalar(tb["cosw"][:], tb["cosw"][:], unscale, None, ALU.mult))
            wr, wi = raw
            link(V.tensor_copy(aa[:, 0, 0], wr[:, :, 1]))
            link(V.tensor_copy(aa[:, 1, 0], wi[:, :, 1]))
            link(V.tensor_tensor(aa[:, 0, 1], wr[:, :, 0], wr[:, :, 2], ALU.add))
            link(V.tensor_tensor(aa[:, 1, 1], wi[:, :, 0], wi[:, :, 2], ALU.add))
            link(V.tensor_tensor(aa[:, 0, 2], wi[:, :, 0], wi[:, :, 2], ALU.subtract))
            link(V.tensor_tensor(aa[:, 1, 2], wr[:, :, 2], wr[:, :, 0], ALU.subtract))
            ar, ai = aa[:, 0], aa[:, 1]

            def combine(dst, re, im, sr, si):
                def pair(j, a, op, sign):
                    if sign > 0 or op == ALU.subtract:
                        u, v = (0, 2) if sign > 0 else (2, 0)
                        link(V.tensor_tensor(dst(j), a[..., u], a[..., v], op))
                    else:
                        link(V.scalar_tensor_tensor(dst(j), a[..., 0], -1.0, a[..., 2], ALU.mult, ALU.subtract))
                link(V.tensor_scalar(dst(0), re[..., 1], float(sr), None, ALU.mult))
                link(V.tensor_scalar(dst(1), im[..., 1], float(-si), None, ALU.mult))
                pair(2, re, ALU.add, sr)
                pair(3, im, ALU.add, -si)
                pair(4, im, ALU.subtract, si)
                pair(5, re, ALU.subtract, sr)

            combine(lambda j: base[:, :, j], ar, ai, 1, 1)
            for j in range(6):
                def rowwise(f):
                    return base[:, f, j].unsqueeze(1).broadcast_to([P, T, C])

                def trig(f):
                    return tb["trig_h"][:, f].unsqueeze(2).broadcast_to([P, T, C])
                link(V.tensor_tensor(scr, rowwise(1), trig(0), ALU.mult))
                link(V.tensor_tensor(sfull, scr, rowwise(0), ALU.add))
                link(V.tensor_tensor(scr, rowwise(2), trig(1), ALU.mult))
                link(V.tensor_tensor(sfull, scr, sfull, ALU.add))
                link(V.tensor_copy(smat[:, :, j], sfull))
                link(V.tensor_tensor(smat[:, :, 6 + j], sfull, smat[:, :, j], ALU.subtract))
            for blk, krow, col, swap, sr, si in ((0, 0, 1, False, 1, 1), (0, 0, 2, True, 1, -1),
                                                 (1, 2, 0, False, 1, 1), (2, 2, 0, True, -1, 1)):
                rows = slice(32 * blk, 32 * blk + C)
                re, im = (a[rows, :, krow] for a in (vraw[::-1] if swap else vraw))
                combine(lambda j: spaced[rows, j, col * C:(col + 1) * C], re, im, sr, si)
            link(V.tensor_copy(spaced16[:, 0:6], spaced))
            V.tensor_tensor(spaced16[:, 6:12], spaced, spaced16[:, 0:6], ALU.subtract).then_inc(vmat_spaced, 1)
            link(V.tensor_scalar(bias_row[:], hker, bcol[:, 1:2], -1.0, ALU.mult, ALU.mult))
            link(V.tensor_tensor(bias_row[:, 0:1], bias_row[:, 0:1], bcol[:, 0:1], ALU.add))
            for primed in (t1_done, t2_done, x1_done, xt_kept, q3_done, p0_ready, qx_done, uv_summed,
                           h_split, base_done, edge_kept,
                           row_out, *stored):
                dve.sem_inc(primed, PRIMED)
            V.memset(sc[:, 16:17], 0.0).then_inc(setup_done, 1)

            links = [0]

            def statistics(n, b):
                def lk(ins):
                    links[0] += 1
                    ins.then_inc(chain, 1)
                    dve.wait_ge(chain, b * LINKS + links[0])
                V.memset(sc[:, 19:20], 0.0)
                V.bn_aggr(sc[:, 0:2], stat[:].rearrange("p t s -> p (t s)")).then_inc(s_mean, 1)
                dve.wait_ge(s_gmean, n)
                dve.wait_ge(s_mean, n)
                lk(V.tensor_copy(sc[:, 6:7], c_ps[:, 16:17]))
                lk(V.tensor_tensor(sc[:, 2:3], sc[:, 0:1], sc[:, 6:7], ALU.subtract))
                V.scalar_tensor_tensor(sc[:, 3:4], sc[:, 2:3], sc[:, 2:3], sc[:, 1:2],
                                       ALU.mult, ALU.add).then_inc(s_dev, 1)
                dve.wait_ge(s_gvar, n)
                V.tensor_scalar(sc[:, 4:5], c_ps[:, 17:18], EPS, None, ALU.add).then_inc(s_var, 1)
                dve.wait_ge(s_sd, n)
                dve.wait_ge(s_var, n)
                lk(V.reciprocal(sc[:, 7:8], sc[:, 5:6]))
                lk(V.scalar_tensor_tensor(sc[:, 11:12], sc[:, 7:8], sc[:, 7:8], sc[:, 4:5], ALU.mult, ALU.mult))
                lk(V.tensor_scalar(sc[:, 11:12], sc[:, 11:12], -0.5, 1.5, ALU.mult, ALU.add))
                lk(V.tensor_tensor(sc[:, 7:8], sc[:, 7:8], sc[:, 11:12], ALU.mult))
                lk(V.tensor_scalar(sc[:, 8:9], sc[:, 7:8], ROW_SCALE, None, ALU.mult))
                lk(V.scalar_tensor_tensor(sc[:, 9:10], sc[:, 8:9], -1.0, sc[:, 6:7], ALU.mult, ALU.mult))
                lk(V.tensor_scalar(sc[:, 10:11], sc[:, 7:8], 1.0 / (K * K), None, ALU.mult))
                lk(V.scalar_tensor_tensor(sc[:, 14:15], sc[:, 10:11], -1.0, sc[:, 6:7], ALU.mult, ALU.mult))
                V.tensor_scalar(box_bias[:], tb["row_count"][:], sc[:, 14:15], None,
                                ALU.mult).then_inc(s_scale, 1)

            LINKS = 2 * 10 + 5

            def count_rows(b, k, r):
                dve.wait_ge(loaded[k], b * 16 + 16)
                V.bn_stats(stat[:, r + k * CHUNK, :], img[:, r + k * CHUNK, :]).then_inc(rows_counted, 1)

            def layer0(b):
                links[0] = 0

                def lk(ins):
                    links[0] += 1
                    ins.then_inc(chain, 1)
                    dve.wait_ge(chain, b * LINKS + links[0])

                dve.wait_ge(rows_counted, (b + 1) * T)
                statistics(b * 2 + 1, b)
                dve.wait_ge(s_vsc_ps, b + 1)
                V.tensor_copy(sc[0:NV, 12:13], c_ps[0:NV, 18:19])
                V.memset(sc[:, 13:14], 0.0)
                lk(V.memset(sc[:, 15:16], 0.0))
                V.tensor_copy(sc[0:C, 13:14], c_ps[0:C, 19:20]).then_inc(s_vscale, 1)
                def split_g(s, done, n, rows=P):
                    dve.wait_ge(g_done if rows == P else vg_done, n + 1)
                    V.tensor_tensor(gp[s][0:rows, 1, :], g32[0:rows], gp[s][0:rows, 0, :],
                                    ALU.subtract).then_inc(done, 1)

                def split_h(s, kept, done, n, rows=P):
                    dve.wait_ge(kept, n + 1)
                    V.scalar_tensor_tensor(hp[s][0:rows, 1, :, 0:HALF + NZ], h_ps[0:rows, :, 0:HALF + NZ],
                                           1.0 / TAB_SCALE, hp[s][0:rows, 0, :, 0:HALF + NZ],
                                           ALU.mult, ALU.subtract).then_inc(done, 1)

                for s in range(NS):
                    dve.wait_ge(stored[s], PRIMED + b * (16 * T // (2 * NS)))
                split_g(0, vg_split, b, NV)
                split_h(0, vh_kept, vh_split, b, NV)
                dve.wait_ge(v_mixed, b + 1)

                def term(dst, pt, cc, wave, rows):
                    for a in range(2):
                        ins = V.scalar_tensor_tensor(dst[0:rows, a, :], pt[0:rows, a * HALF:(a + 1) * HALF],
                                                     edge[0:rows, cc + a:cc + a + 1], wave[0:rows, a, :],
                                                     ALU.add, ALU.mult)
                    return ins
                lk(V.tensor_copy(edge[0:NV, 0:6], c_ps[0:NV, 0:6]))
                term(t1, p1, 4, cosw, NV)
                lk(term(t2, p2, 0, sinw, NV))
                lk(V.tensor_tensor(t1[0:NV], t1[0:NV], t2[0:NV], ALU.add))
                for a in range(2):
                    ins = V.tensor_scalar(base0[0:NV, a, :], p0[0:NV, a * HALF:(a + 1) * HALF],
                                          edge[0:NV, 2 + a:3 + a], unscale[0:NV], ALU.add, ALU.mult)
                lk(ins)
                V.tensor_tensor(qx[0:NV], base0[0:NV], t1[0:NV], ALU.add).then_inc(v_rows, 1)
                dve.wait_ge(v_spread, b + 1)
                for j, pt in enumerate((p0, p1, p2)):
                    ins = V.tensor_copy(rmap[:, j], halves(pt[:]))
                ins.then_inc(v_maps, 1)
                dve.wait_ge(v_maps, b + 1)
                assert links[0] <= LINKS

                def wrap_first(t, s):
                    V.scalar_tensor_tensor(wadd[s], rmap[:, 1], tb["trig_h"][:, 0, bass.ds(t, 1)], rmap[:, 0],
                                           ALU.mult, ALU.add).then_inc(wa_done, 1)

                def wrap_second(n, t, s):
                    dve.wait_ge(wa_done, n + 1)
                    V.scalar_tensor_tensor(wadd[s], rmap[:, 2], tb["trig_h"][:, 1, bass.ds(t, 1)], wadd[s],
                                           ALU.mult, ALU.add).then_inc(w_done, 1)

                def spread(t, s):
                    V.tensor_tensor(bd[s], smat[:, t, :, :].unsqueeze(2).broadcast_to([P, 12, HB, C]),
                                    tb["hb_mask16"][:].unsqueeze(1).broadcast_to([P, 12, HB, C]),
                                    ALU.mult).then_inc(bd_ready, 1)

                def row(n, t, s, spread_ahead=True, wrap_ahead=True):
                    dve.wait_ge(edge_ready, n + 1)
                    dve.wait_ge(base_done, PRIMED + n)
                    V.tensor_copy(edge[:, 0:6], c_ps[:, 0:6])
                    V.tensor_scalar(edge[:, 6:8], c_ps[:, 2:4], unscale, None, ALU.mult).then_inc(edge_kept, 1)
                    dve.wait_ge(edge_kept, PRIMED + n + 1)
                    dve.wait_ge(p1_ready, n + 1)
                    dve.wait_ge(q3_done, PRIMED + n)
                    term(t1, p1, 4, cosw, P).then_inc(t1_done, 1)
                    dve.wait_ge(p2_ready, n + 1)
                    term(t2, p2, 0, sinw, P).then_inc(t2_done, 1)
                    if wrap_ahead:
                        wrap_first(t + 1, 1 - s)
                    if spread_ahead:
                        dve.wait_ge(p0_ready, PRIMED + n + 1)
                        spread(t + 2, s)
                    if wrap_ahead:
                        wrap_second(n + 1, t + 1, 1 - s)
                        split_h(1 - s, h_kept, h_split, n + 1)
                    dve.wait_ge(base_done, PRIMED + n + 1)
                    dve.wait_ge(q3_done, PRIMED + n + 1)
                    V.tensor_tensor(parity(img[:, t, :]), base0[:], qx, ALU.add).then_inc(x1_done, 1)
                    dve.wait_ge(x1_done, PRIMED + n + 1)
                    V.bn_stats(stat[:, t, :], img[:, t, :]).then_inc(x1_counted, 1)

                spread(0, 0)
                spread(1, 1)
                dve.wait_ge(qx_done, PRIMED + b * T)
                wrap_first(0, 0)
                wrap_second(b * T, 0, 0)
                dve.wait_ge(g_done, b * T + 1)
                V.tensor_tensor(img[:, 0, :], img[:, 0, :], bias_row[:], ALU.add).then_inc(bias_added, 1)
                split_h(0, h_kept, h_split, b * T)
                with dve.Fori(0, T // 2 - 1) as i:
                    for s in range(2):
                        row(b * T + i * 2 + s, i * 2 + s, s)
                row(b * T + T - 2, T - 2, 0, spread_ahead=False)
                row(b * T + T - 1, T - 1, 1, spread_ahead=False, wrap_ahead=False)
                dve.wait_ge(x1_counted, (b + 1) * T)
                statistics(b * 2 + 2, b)
                assert links[0] == LINKS, links[0]

            def layer1(b, follow):
                for s in range(2):
                    V.memset(padded[s][:, 0:K], 0.0)
                    ins = V.memset(padded[s][:, K + W:PADW], 0.0)
                ins.then_inc(pads_zero, 1)
                dve.wait_ge(pads_zero, b + 1)

                def run_sum(n, s):
                    dve.wait_ge(row_padded[0], n + 1)
                    dve.wait_ge(row_padded[1], n + 1)
                    V.tensor_tensor_scan(sums[s], padded[s][:, K:K + SUMW], padded[s][:, 0:SUMW], 0.0,
                                         ALU.add, ALU.subtract).then_inc(row_summed, 1)

                def difference(t, s):
                    dve.wait_ge(col_summed[1], b * T + t)
                    V.tensor_tensor(diff[s], img[:, t + (R + 1), :], img[:, t - R, :],
                                    ALU.subtract).then_inc(moved, 1)

                def steps(lo, hi, diffs):
                    with dve.Fori(lo // 2, hi // 2) as i:
                        for s in range(2):
                            dve.wait_ge(row_out, PRIMED + b * T + i * 2 + (s - 1))
                            run_sum(b * T + i * 2 + s, s)
                            if diffs:
                                difference(i * 2 + (s + 2), s)

                for s in range(2):
                    run_sum(b * T + s, s)
                steps(2, R - 1, False)
                difference(R, 1)
                steps(R - 1, T // 2, True)
                for q in range(AHEAD):
                    for r in range(CHUNK):
                        t = T - CHUNK * (AHEAD - q) + r
                        dve.wait_ge(row_out, PRIMED + b * T + t - 1)
                        run_sum(b * T + t, t % 2)
                        if t + 2 < T - R - 1:
                            difference(t + 2, t % 2)
                        if follow:
                            count_rows(b + 1, q + 1, r)
                if follow:
                    for k in [*range(AHEAD + 1, NCH), 0]:
                        with dve.Fori(0, CHUNK) as r:
                            count_rows(b + 1, k, r)

            for k in [*range(1, NCH), 0]:
                with dve.Fori(0, CHUNK) as r:
                    count_rows(0, k, r)
            with dve.Fori(0, B - 1) as b:
                layer0(b)
                layer1(b, True)
            layer0(B - 1)
            layer1(B - 1, False)

        @block.gpsimd
        def _(pool):
            G = nc.gpsimd
            pool.wait_ge(max_w, 1)
            G.partition_all_reduce(sc[:, 1:2], sc[:, 0:1], P, bass.bass_isa.ReduceOp.max).then_inc(max_all, 1)
            pool.wait_ge(setup_done, 1)
            pool.wait_ge(tab_in, 16 * len(TABLES))
            def sum_weights(b, q, s):
                if q == 0:
                    pool.wait_ge(uv_summed, PRIMED + b * (T // 4))
                else:
                    pool.wait_ge(uv_summed, PRIMED + b * (T // 4) + (2 * q + s - 1))
                t = (q + 1) % NCH * CHUNK + 4 * s
                rows = tb["virt_h"][:, t:t + 4, :].rearrange("p t j -> p (t j)")
                G.tensor_tensor(uvw[s][:, :, 0:C], rows.unsqueeze(2).broadcast_to([P, 12, C]),
                                tb["c_mask"][:].unsqueeze(1).broadcast_to([P, 12, C]),
                                ALU.mult).then_inc(uvw_ready, 1)

            def layer0(b):
                def split_g(n, s):
                    pool.wait_ge(g_done, n + 1)
                    G.tensor_tensor(gp[s][:, 1, :], g32, gp[s][:, 0, :], ALU.subtract).then_inc(g_split, 1)

                def add_row(n, t, s):
                    pool.wait_ge(w_done, n + 1)
                    pool.wait_ge(x1_done, PRIMED + n)
                    G.tensor_tensor(qx, wadd[s], parity(img[:, t, :]), ALU.add).then_inc(qx_done, 1)

                def add_terms(n):
                    pool.wait_ge(t2_done, PRIMED + n + 1)
                    G.tensor_tensor(t1, t1, t2, ALU.add).then_inc(q_done, 1)
                    pool.wait_ge(q_done, n + 1)
                    pool.wait_ge(qx_done, PRIMED + n + 1)
                    G.tensor_tensor(qx, qx, t1, ALU.add).then_inc(q3_done, 1)

                split_g(b * T, 0)
                pool.wait_ge(bias_added, b + 1)
                split_g(b * T + 1, 1)
                add_row(b * T, 0, 0)
                with pool.Fori(0, T // 2 - 1) as i:
                    for s in range(2):
                        n = b * T + i * 2 + s
                        split_g(n + 2, s)
                        add_terms(n)
                        add_row(n + 1, i * 2 + (s + 1), 1 - s)
                add_terms(b * T + T - 2)
                add_row(b * T + T - 1, T - 1, 1)
                add_terms(b * T + T - 1)

            def layer1(b, follow):
                def two_rows(i, s):
                    pool.wait_ge(stored[s], PRIMED + (b * (T // (2 * NS)) + i) * 16)
                    for r in range(2):
                        t = i * (2 * NS) + (2 * s + r)
                        pool.wait_ge(row_summed, b * T + t + 1)
                        G.tensor_tensor(ob[s][:, r, :], sums[r][:, R:R + W], img[:, t, :],
                                        ALU.add).then_inc(row_out, 1)

                with pool.Fori(0, T // 2 // (2 * NS)) as i:
                    for s in range(NS):
                        two_rows(i, s)
                if follow:
                    for s in range(2):
                        sum_weights(b + 1, 0, s)
                for j in range(T // 8, T // 4):
                    for s in range(2):
                        two_rows(j // 2, 2 * (j % 2) + s)
                    if follow:
                        q, s = divmod(j - T // 8 + 2, 2)
                        sum_weights(b + 1, q, s)
                if follow:
                    for j in range(2 * AHEAD + 2, 2 * NCH):
                        sum_weights(b + 1, j // 2, j % 2)

            for q in range(NCH):
                for s in range(2):
                    sum_weights(0, q, s)
            with pool.Fori(0, B - 1) as b:
                layer0(b)
                layer1(b, True)
            layer0(B - 1)
            layer1(B - 1, False)


_INS = ["x", "L0_conv_w_real", "L0_conv_w_imag", "L0_conv_b_real", "L0_conv_b_imag"]


def kernel(**inputs):
    import concourse.bacc as bacc
    from concourse.bass_utils import run_bass_kernel_spmd

    nc = bacc.Bacc("TRN2", target_bir_lowering=False, num_devices=1)
    arrays, args = {}, []
    for name in _INS:
        a = np.ascontiguousarray(inputs[name])
        arrays[f"in_{name}"] = a
        args.append(nc.dram_tensor(f"in_{name}", a.shape, mybir.dt.from_np(a.dtype), kind="ExternalInput").ap())
    tab = {}
    for name, a in tables().items():
        arrays[f"tab_{name}"] = a
        tab[name] = nc.dram_tensor(f"tab_{name}", a.shape, mybir.dt.from_np(a.dtype), kind="ExternalInput").ap()
    out = nc.dram_tensor("out_0", (B, C, H, W), F32, kind="ExternalOutput").ap()
    build(nc, *args, tab, out)
    r = run_bass_kernel_spmd(nc, [arrays], core_ids=[0])
    return r.results[0]["out_0"]
```

```python
from contextlib import ExitStack

import numpy as np

import concourse.bass as bass
from concourse import mybir

F32 = mybir.dt.float32
F16 = mybir.dt.float16
ALU = mybir.AluOpType
ACT = mybir.ActivationFunctionType

P = 128
B, C, H, W = 8, 16, 512, 512
HB = P // C
T = H // HB
GROUP = 2 * HB
HALF = W // 2
NZ = 5
HZ = HALF + 8
K = 15
R = K // 2
EPS = 1e-5
CHUNK = 8
NCH = T // CHUNK
PADW = K + W + R
SUMW = W + R
NDIFF = T - K
AHEAD = NCH // 2
PRIMED = 1
ROW_SCALE = 32.0
MAT_SCALE = 2048.0
TAB_SCALE = 65536.0
NS = 4
NV = 3 * C
QUARTER = HALF // 4

TABLES = ["ident", "prev", "next_", "neg_ident", "neg_prev", "group_mean", "cosw",
          "to_virtual", "from_virtual", "c_mask", "trig_h", "virt_h", "row_count", "hilbert_kernel",
          "ident16", "hb_mask16", "hilbert16"]


def tables():
    th = 2 * np.pi / W
    p = np.arange(P)
    hb, c = p // C, p % C
    h = (hb[:, None] * T + np.arange(T)[None, :])
    eye = np.eye(P)
    prev = np.zeros((P, P))
    nxt = np.zeros((P, P))
    for m in range(P):
        if hb[m] != 0:
            prev[m - C, m] = 1
        if hb[m] != HB - 1:
            nxt[m + C, m] = 1

    def kern(n):
        n = np.asarray(n)
        odd = n % 2 == 1
        return np.where(odd, 2.0 / W / np.tan(np.pi * np.where(odd, n, 1) / W), 0.0)

    def split(v):
        high = v.astype(np.float16)
        return np.stack([high, (v - high).astype(np.float16)], 1)

    hil = np.zeros((P, 4, HALF + NZ))
    for k in range(4):
        par, half = k // 2, k % 2
        w = 2 * (P * half + np.arange(P)) + par
        wo = 2 * np.arange(HALF) + (1 - par)
        hil[:, k, :HALF] = kern(wo[None, :] - w[:, None])
        hil[:, k, HALF + 0] = 2.0 / W
        hil[:, k, HALF + 1] = np.sin(th * w) / W
        hil[:, k, HALF + 2] = -np.cos(th * w) / W
        hil[:, k, HALF + 3] = -2.0 / W
        hil[:, k, HALF + 4] = -np.sin(th * w) / W
    wsep = np.stack([2 * np.arange(-QUARTER, HALF), 2 * np.arange(-QUARTER, HALF) + 1])
    tov = np.zeros((P, NV))
    fromv = np.zeros((NV, 3, P))
    for cc in range(C):
        for j in range(3):
            tov[cc, j * C + cc] = 1
            fromv[j * C + cc, j, cc::C] = -1
    trig = np.stack([np.cos(th * h), np.sin(th * h)], 1)
    virt = np.stack([np.ones_like(h) / H, np.cos(th * h) / H, np.sin(th * h) / H], 2)
    count = np.minimum(h + R, H - 1) - np.maximum(h - R, 0) + 1
    count = count[:, [*range(R + 1), *range(T - R - 1, T)]]
    out = {
        "ident": eye, "prev": prev, "next_": nxt, "neg_ident": -eye, "neg_prev": -prev,
        "group_mean": (c[:, None] // 2 == c[None, :] // 2) / GROUP,
        "hilbert16": split(hil * TAB_SCALE),
        "cosw": np.broadcast_to(np.cos(th * wsep), (P, *wsep.shape)),
        "to_virtual": tov, "from_virtual": fromv,
        "ident16": eye,
        "hb_mask16": np.broadcast_to((hb[:, None] == np.arange(HB)[None, :])[:, :, None], (P, HB, C)),
        "c_mask": c[:, None] == np.arange(C)[None, :],
        "trig_h": trig, "virt_h": virt, "row_count": count,
        "hilbert_kernel": np.tile(kern(np.arange(W)), (P, 1)),
    }
    return {k: np.ascontiguousarray(v, dtype=np.float16 if k.endswith("16") else np.float32)
            for k, v in out.items()}


def build(nc, x, w_real, w_imag, b_real, b_imag, tab, out):
    x_v = x.rearrange("b c (hb t) w -> b hb c (t w)", hb=HB)
    out_v = out.rearrange("b c (hb t) w -> b hb c (t w)", hb=HB)
    with ExitStack() as ctx:
        def sb(name, shape, dt=F32):
            return ctx.enter_context(nc.sbuf_tensor(name, shape, dt))

        def sem(name):
            return ctx.enter_context(nc.semaphore(name))

        img = sb("img", [P, T, W])
        smat = sb("smat", [P, T, 12, C], F16)
        tb = {n: sb(n, list(tab[n].shape), tab[n].dtype) for n in TABLES if n != "hilbert_kernel"}
        vmat = sb("vmat", [NV, 12, NV], F16)
        uvw = [sb(f"uvw{s}", [P, 4 * 3, C]) for s in range(2)]
        rmap = sb("rmap", [P, 3, 2, HALF])
        bias_row = sb("bias_row", [P, W])
        cosw, sinw = tb["cosw"][:, :, QUARTER:], tb["cosw"][:, :, 0:HALF]
        sizes = [W, W, W, W, 2 * HZ, 2 * HZ]
        work = sb("work", [P, sum(sizes)])
        at = np.cumsum([0] + sizes)
        piece = [work[:, int(at[i]):int(at[i + 1])] for i in range(len(sizes))]
        g32 = piece[0]
        gp = [piece[1 + s].bitcast(F16).rearrange("p (l j) -> p l j", l=2) for s in range(2)]
        xT = piece[3].bitcast(F16).rearrange("p (k m) -> p k m", k=8)
        hp = [piece[4 + s].bitcast(F16).rearrange("p (l a n) -> p l a n", l=2, a=2) for s in range(2)]
        padded = [work[:, s * PADW:(s + 1) * PADW] for s in range(2)]
        sums = [work[:, 2 * PADW + s * SUMW:2 * PADW + (s + 1) * SUMW] for s in range(2)]
        assert 2 * (PADW + SUMW) <= sum(sizes)
        ob = [sb(f"ob{s}", [P, 2, W]) for s in range(2)]
        t1, t2 = (ob[0][:, i, :].rearrange("p (a j) -> p a j", a=2) for i in range(2))
        wadd = [ob[1][:, i, :].rearrange("p (a j) -> p a j", a=2) for i in range(2)]
        more = sb("more", [P, 4 * W])
        ob += [more[:, i * 2 * W:(i + 1) * 2 * W].rearrange("p (r w) -> p r w", r=2) for i in range(2)]
        bd = [more[:, s * 6 * P:(s + 1) * 6 * P].bitcast(F16).rearrange("p (j h c) -> p j h c", j=12, h=HB)
              for s in range(2)]
        qx = more[:, 12 * P:16 * P].rearrange("p (a j) -> p a j", a=2)
        base0 = sb("base0", [P, 2, HALF])
        edge = sb("edge", [P, 8])
        diff = [rmap[:, s] .rearrange("p a j -> p (a j)") for s in range(2)]
        stat = sb("stat", [P, T, 6])
        sc = sb("sc", [P, 24])
        box_bias = sb("box_bias", [P, 2 * (R + 1)])

        xt_ps = ctx.enter_context(nc.psum_tensor("xt_ps", [P, 8, P], F16))
        h_ps = ctx.enter_context(nc.psum_tensor("h_ps", [P, 2, W], F32))
        p0 = ctx.enter_context(nc.psum_tensor("p0", [P, W], F32))
        p1 = ctx.enter_context(nc.psum_tensor("p1", [P, W], F32))
        p2 = ctx.enter_context(nc.psum_tensor("p2", [P, W], F32))
        c_ps = ctx.enter_context(nc.psum_tensor("c_ps", [P, W], F32))
        uv_ps = ctx.enter_context(nc.psum_tensor("uv_ps", [P, W], F32))

        tab_in, w_in, zeroed = sem("tab_in"), sem("w_in"), sem("zeroed")
        setup_chain, setup_done = sem("setup_chain"), sem("setup_done")
        vmat_spaced, vmat_in = sem("vmat_spaced"), sem("vmat_in")
        loaded = [sem(f"loaded{k}") for k in range(NCH)]
        uvw_ready, uv_summed, rows_counted = sem("uvw_ready"), sem("uv_summed"), sem("rows_counted")
        chain = sem("chain")
        s_mean, s_gmean, s_dev, s_gvar = sem("s_mean"), sem("s_gmean"), sem("s_dev"), sem("s_gvar")
        s_var, s_sd, s_scale, s_vsum, s_vscale = (sem("s_var"), sem("s_sd"), sem("s_scale"),
                                                    sem("s_vsum"), sem("s_vscale"))
        vg_done, vxt_made, vxt_kept, vh_made, vh_kept = (sem("vg_done"), sem("vxt_made"), sem("vxt_kept"),
                                                         sem("vh_made"), sem("vh_kept"))
        v_mixed, v_rows, v_spread, v_maps = sem("v_mixed"), sem("v_rows"), sem("v_spread"), sem("v_maps")
        v_map_sin = sem("v_map_sin")
        g_done, xt_made, xt_kept, h_made, h_kept = (sem("g_done"), sem("xt_made"), sem("xt_kept"),
                                                    sem("h_made"), sem("h_kept"))
        bd_ready, p1_ready, p2_ready, p0_ready = sem("bd_ready"), sem("p1_ready"), sem("p2_ready"), sem("p0_ready")
        t1_done, t2_done, t1_added, terms_added = sem("t1_done"), sem("t2_done"), sem("t1_added"), sem("terms_added")
        wrap_begun, wrap_done, qx_done, x1_done = sem("wrap_begun"), sem("wrap_done"), sem("qx_done"), sem("x1_done")
        bias_added, x1_counted = sem("bias_added"), sem("x1_counted")
        moved = sem("moved")
        vg_split, vh_split, g_split, h_split = sem("vg_split"), sem("vh_split"), sem("g_split"), sem("h_split")
        g_used, edge_ready, edge_kept, base_done = sem("g_used"), sem("edge_ready"), sem("edge_kept"), sem("base_done")
        base_ready, pool_matrices = sem("base_ready"), sem("pool_matrices")
        max_w, max_all = sem("max_w"), sem("max_all")
        pads_zero, row_summed, row_out = sem("pads_zero"), sem("row_summed"), sem("row_out")
        col_summed = [sem(f"col_summed{a}") for a in range(2)]
        row_padded = [sem(f"row_padded{a}") for a in range(2)]
        stored = [sem(f"stored{s}") for s in range(NS)]

        flat = img[:, 0:CHUNK, :].rearrange("p t w -> p (t w)")
        raw = [flat[:, i * 144:(i + 1) * 144].rearrange("p (o a b) -> p o a b", o=C, a=3) for i in range(2)]
        vraw = [flat[:, (2 + i) * 144:(3 + i) * 144].rearrange("p (o a b) -> p o a b", o=C, a=3)
                for i in range(2)]
        aa = flat[:, 576:864].rearrange("p (r f o b) -> p r f o b", r=2, f=3, o=C)
        base = flat[:, 864:1152].rearrange("p (f j o) -> p f j o", f=3, j=6)
        spaced = flat[:, 1152:1152 + 6 * NV].rearrange("p (j m) -> p j m", j=6)
        spaced16 = flat[:, 1440:1440 + 6 * NV].bitcast(F16).rearrange("p (j m) -> p j m", j=12)
        scratch = [flat[:, 2048 + i * T * C:2048 + (i + 1) * T * C].rearrange("p (t o) -> p t o", o=C)
                   for i in range(2)]
        scratch_g = [ob[i].rearrange("p r w -> p (r w)")[:, 0:T * C].rearrange("p (t o) -> p t o", o=C)
                     for i in range(2)]
        assert 1440 + 6 * NV <= 2048 and 2048 + 2 * T * C <= CHUNK * W and T * C <= 2 * W
        unscale = sc[:, 22:23]
        bcol = sc[:, 20:22]

        def parity(ap):
            return ap.rearrange("p (j two) -> p two j", two=2)

        def halves(ap):
            return ap.rearrange("p (a j) -> p a j", a=2)

        def row_matrices(engine, link, room, terms):
            scr, full = room
            for j in terms:
                def part(f):
                    return base[:, f, j].unsqueeze(1).broadcast_to([P, T, C])

                def trig(f):
                    return tb["trig_h"][:, f].unsqueeze(2).broadcast_to([P, T, C])
                link(engine.tensor_tensor(scr, part(1), trig(0), ALU.mult))
                link(engine.tensor_tensor(full, scr, part(0), ALU.add))
                link(engine.tensor_tensor(scr, part(2), trig(1), ALU.mult))
                link(engine.tensor_tensor(full, scr, full, ALU.add))
                link(engine.tensor_copy(smat[:, :, j], full))
                link(engine.tensor_tensor(smat[:, :, 6 + j], full, smat[:, :, j], ALU.subtract))

        block = ctx.enter_context(nc.Block())

        @block.sync
        def _(sp):
            for n in TABLES:
                dst = bias_row[:] if n == "hilbert_kernel" else tb[n][:]
                sp.dma_start(dst, tab[n]).then_inc(tab_in, 16)
            sp.wait_ge(zeroed, 1)
            for i, wr in enumerate((w_real, w_imag)):
                w_flat = wr.rearrange("i o a b -> i (o a b)")
                for k in range(HB):
                    sp.dma_start(flat[k * C:(k + 1) * C, i * 144:(i + 1) * 144], w_flat).then_inc(w_in, 16)
                for k in range(3):
                    sp.dma_start(flat[32 * k:32 * k + C, (2 + i) * 144:(3 + i) * 144], w_flat).then_inc(w_in, 16)
            for i, br in enumerate((b_real, b_imag)):
                sp.dma_start(sc[0:C, 20 + i:21 + i], br.rearrange("(c o) -> c o", o=1)).then_inc(w_in, 16)

            def load(b, k):
                sp.dma_start(img[:, k * CHUNK:(k + 1) * CHUNK, :].rearrange("p t w -> p (t w)"),
                             x_v[b, :, :, k * CHUNK * W:(k + 1) * CHUNK * W]).then_inc(loaded[k], 16)

            def store(b, j, s):
                sp.wait_ge(row_out, PRIMED + b * T + j * 2 + 2)
                sp.dma_start(out_v[b, :, :, bass.ds(j * (2 * W), 2 * W)],
                             ob[s][:].rearrange("p t w -> p (t w)")).then_inc(stored[s], 16)

            for k in range(1, NCH):
                load(0, k)
            sp.wait_ge(vmat_spaced, 1)
            for k in range(3):
                sp.dma_start(vmat[k * C:(k + 1) * C, :, :].rearrange("p j m -> p (j m)"),
                             spaced16[32 * k:32 * k + C, :, :].rearrange("p j m -> p (j m)")).then_inc(vmat_in, 16)
            sp.wait_ge(vmat_in, 48)
            sp.wait_ge(setup_done, 1)
            load(0, 0)

            with sp.Fori(0, B - 1) as b:
                for j in range(8):
                    store(b, j, j % NS)
                for k in range(1, NCH - 1):
                    for j in range(4 * k + 4, 4 * k + 8):
                        store(b, j, j % NS)
                    sp.wait_ge(col_summed[1], b * T + CHUNK * (k + 1) + R + 1)
                    load(b + 1, k)
                for k in (NCH - 1, 0):
                    load(b + 1, k)
            with sp.Fori(0, T // (2 * NS)) as i:
                for s in range(NS):
                    store(B - 1, i * NS + s, s)
            for s in range(NS):
                sp.wait_ge(stored[s], PRIMED + 16 * B * T // (2 * NS))

        @block.tensor
        def _(pe):
            mm = nc.tensor.matmul
            pe.wait_ge(tab_in, 16 * len(TABLES))

            def group_mean(n):
                pe.wait_ge(s_mean, n)
                mm(c_ps[:, 16:17], tb["group_mean"][:], sc[:, 0:1], start=True, stop=True).then_inc(s_gmean, 1)

            def group_variance(n):
                pe.wait_ge(s_dev, n)
                mm(c_ps[:, 17:18], tb["group_mean"][:], sc[:, 3:4], start=True, stop=True).then_inc(s_gvar, 1)

            def hold():
                nc.tensor.transpose(xt_ps[:, 0, :], tb["ident16"][:], tb["ident16"][:])

            def turn(parts, rows=P):
                for l in range(2):
                    for k in range(4):
                        m = nc.tensor.transpose(xt_ps[:, 4 * l + k, 0:rows], parts[0:rows, l, k * P:(k + 1) * P],
                                                tb["ident16"][0:rows, 0:rows])
                return m

            def hilbert(rows=P):
                for a in range(2):
                    for half in range(2):
                        k = 2 * (1 - a) + half
                        for i, (lx, lt) in enumerate(((0, 0), (0, 1), (1, 0))):
                            m = mm(h_ps[0:rows, a, 0:HALF + NZ], xT[:, 4 * lx + k, 0:rows],
                                   tb["hilbert16"][:, lt, k, :], start=(half == 0 and i == 0),
                                   stop=(half == 1 and i == 2))
                return m

            def product(dst, mat, j, parts, start, stop):
                for i, (lm, lp) in enumerate(((0, 0), (0, 1), (1, 0))):
                    m = mm(dst, mat(6 * lm + j), parts(lp), start=start and i == 0, stop=stop and i == 2)
                return m

            def edge_terms(mat, hrow, rows):
                def add(c0, c1, j, z, first, last):
                    for i, (lm, lp) in enumerate(((0, 0), (0, 1), (1, 0))):
                        m = mm(c_ps[0:rows, c0:c1], mat(6 * lm + j), z(lp), start=first and i == 0,
                               stop=last and i == 2, skip_group_check=True)
                    return m
                row = hrow[0:rows]

                def opp(f):
                    return lambda l: row[:, l, :, HALF + f:HALF + f + 2].rearrange("p a f -> p f a")

                def same(f):
                    return lambda l: row[:, l, ::-1, HALF + f:HALF + f + 1]
                add(0, 4, 3, opp(0), True, False)
                add(2, 6, 5, opp(2), False, False)
                add(2, 4, 2, same(2), False, False)
                return add(2, 4, 4, same(4), False, True)

            def sum_rows(b, q, k, r):
                s = r // 4
                if r == 0:
                    pe.wait_ge(loaded[k], b * 16 + 16)
                if r % 4 == 0:
                    pe.wait_ge(uvw_ready, b * (T // 4) + (2 * q + s + 1))
                w = uvw[s][:, 3 * (r % 4):3 * (r % 4) + 3, :].rearrange("p j c -> p (j c)")
                m = mm(uv_ps[0:NV, :], w, img[:, k * CHUNK + r, :], start=(q == 0 and r == 0),
                       stop=(q == NCH - 1 and r == CHUNK - 1))
                if r % 4 == 3:
                    m.then_inc(uv_summed, 1)
                if q == NCH - 1 and r == 2:
                    group_mean(b * 2 + 1)
                if q == NCH - 1 and r == 4:
                    group_variance(b * 2 + 1)

            def front_turn(n, s):
                pe.wait_ge(g_split, n + 1)
                pe.wait_ge(xt_kept, PRIMED + n)
                turn(gp[s]).then_inc(xt_made, 1)

            def front_hilbert(n, s):
                pe.wait_ge(xt_kept, PRIMED + n + 1)
                pe.wait_ge(h_split, PRIMED + n)
                hilbert().then_inc(h_made, 1)

            def layer0(b):
                pe.wait_ge(s_scale, b * 2 + 1)
                mm(c_ps[0:NV, 18:20], tb["to_virtual"][:], sc[:, 8:10], start=True, stop=True).then_inc(s_vsum, 1)

                def vm(j):
                    return vmat[:, j, :]
                pe.wait_ge(vg_done, b + 1)
                hold()
                pe.wait_ge(vg_split, b + 1)
                hold()
                turn(gp[1], NV).then_inc(vxt_made, 1)
                pe.wait_ge(vxt_kept, b + 1)
                hilbert(NV).then_inc(vh_made, 1)
                front_turn(b * T, 0)
                pe.wait_ge(xt_kept, PRIMED + b * T + 1)
                pe.wait_ge(s_vscale, b + 1)
                hold()
                pe.wait_ge(vh_split, b + 1)
                hold()
                edge_terms(vm, hp[1], NV)
                for pt, jg, jh in ((p1, 2, 3), (p2, 4, 5), (p0, 0, 1)):
                    product(pt[0:NV, :], vm, jg, lambda l: gp[1][0:NV, l, :], True, False)
                    m = product(pt[0:NV, :], vm, jh, lambda l: hp[1][0:NV, l, :, 0:HALF], False, True)
                m.then_inc(v_mixed, 1)
                front_hilbert(b * T, 0)
                pe.wait_ge(v_rows, b + 1)
                for j, pt in enumerate((p0, p1, p2)):
                    m = mm(pt[:], tb["from_virtual"][:, j, :], qx[0:NV, :, :], start=True, stop=True)
                m.then_inc(v_spread, 1)
                pe.wait_ge(v_maps, b + 1)
                pe.wait_ge(v_map_sin, b + 1)
                hold()

                def mix(n, s):
                    def mat(j):
                        return bd[s][:, j].rearrange("p h c -> p (h c)")

                    def g_row(l):
                        return gp[s][:, l, :]

                    def h_row(l):
                        return hp[s][:, l, :, 0:HALF]
                    pe.wait_ge(bd_ready, n + 1)
                    pe.wait_ge(t1_done, PRIMED + n)
                    product(p1[:], mat, 2, g_row, True, False)
                    pe.wait_ge(t2_done, PRIMED + n)
                    product(p2[:], mat, 4, g_row, True, False)
                    pe.wait_ge(base_done, PRIMED + n)
                    product(p0[:], mat, 0, g_row, True, False).then_inc(g_used, 1)
                    pe.wait_ge(h_split, PRIMED + n + 1)
                    pe.wait_ge(edge_kept, PRIMED + n)
                    edge_terms(mat, hp[s], P).then_inc(edge_ready, 1)
                    product(p1[:], mat, 3, h_row, False, True).then_inc(p1_ready, 1)
                    product(p2[:], mat, 5, h_row, False, True).then_inc(p2_ready, 1)
                    product(p0[:], mat, 1, h_row, False, True).then_inc(p0_ready, 1)

                with pe.Fori(0, T // 2 - 1) as i:
                    for s in range(2):
                        n = b * T + i * 2 + s
                        front_turn(n + 1, 1 - s)
                        mix(n, s)
                        front_hilbert(n + 1, 1 - s)
                front_turn(b * T + T - 1, 1)
                mix(b * T + T - 2, 0)
                front_hilbert(b * T + T - 1, 1)
                mix(b * T + T - 1, 1)

                def begin(bank, a, rows):
                    for r in rows:
                        m = mm(bank[:, 0:HALF], tb["ident" if r <= R else "prev"][:],
                               img[:, r, a * HALF:(a + 1) * HALF], start=(r == 0), stop=(r == T - 1),
                               skip_group_check=True)
                    return m
                early = [*range(R + 1), *range(T - R, T - 1)]
                pe.wait_ge(x1_done, PRIMED + b * T + T - 1)
                pe.wait_ge(t1_done, PRIMED + b * T + T)
                begin(p1, 1, early)
                group_mean(b * 2 + 2)
                pe.wait_ge(base_done, PRIMED + b * T + T)
                begin(p0, 0, early[:3])
                group_variance(b * 2 + 2)
                begin(p0, 0, early[3:])
                pe.wait_ge(x1_done, PRIMED + b * T + T)
                for a, bank in enumerate((p0, p1)):
                    begin(bank, a, [T - 1]).then_inc(col_summed[a], 1)

            def layer1(b, follow):
                def move_on(t, *parts):
                    for a, bank in enumerate((p0, p1)):
                        pe.wait_ge(row_padded[a], b * T + t + 1)
                        for i, (mat, row) in enumerate(parts):
                            m = mm(bank[:, 0:HALF], tb[mat][:], row(a), start=False,
                                   stop=(i == len(parts) - 1), skip_group_check=True)
                        m.then_inc(col_summed[a], 1)

                def img_row(t):
                    return lambda a: img[:, t, a * HALF:(a + 1) * HALF]

                def move_diff(t, s):
                    pe.wait_ge(moved, b * NDIFF + t - R + 1)
                    move_on(t, ("ident", lambda a: diff[s][:, a * HALF:(a + 1) * HALF]))

                with pe.Fori(0, R) as t:
                    move_on(t, ("ident", img_row(t + (R + 1))), ("neg_prev", img_row(t + (T - R))))
                move_diff(R, 1)
                with pe.Fori(R // 2 + 1, T // 4) as i:
                    for s in range(2):
                        move_diff(i * 2 + s, s)
                for q in range(AHEAD):
                    for r in range(CHUNK):
                        t = T - CHUNK * (AHEAD - q) + r
                        if t < T - R - 1:
                            move_diff(t, t % 2)
                        elif t < T - 1:
                            move_on(t, ("next_", img_row(t - (T - R - 1))), ("neg_ident", img_row(t - R)))
                        if follow:
                            sum_rows(b + 1, q, q + 1, r)
                if follow:
                    for q in range(AHEAD, NCH):
                        for r in range(CHUNK):
                            sum_rows(b + 1, q, (q + 1) % NCH, r)

            for q in range(NCH):
                if q == NCH - 1:
                    pe.wait_ge(setup_done, 1)
                    pe.wait_ge(vmat_in, 48)
                for r in range(CHUNK):
                    sum_rows(0, q, (q + 1) % NCH, r)
            with pe.Fori(0, B - 1) as b:
                layer0(b)
                layer1(b, True)
            layer0(B - 1)
            layer1(B - 1, False)

        @block.scalar
        def _(act):
            def copy(out_, in_):
                return nc.scalar.activation(out_, in_, ACT.Identity)

            def high_hilbert(s, rows=P):
                return nc.scalar.activation(hp[s][0:rows, 0, :, 0:HALF + NZ], h_ps[0:rows, :, 0:HALF + NZ],
                                            ACT.Identity, scale=1.0 / TAB_SCALE)

            def deviation(n):
                act.wait_ge(s_var, n)
                nc.scalar.activation(sc[:, 5:6], sc[:, 4:5], ACT.Sqrt).then_inc(s_sd, 1)

            act.wait_ge(setup_done, 1)
            with act.Fori(0, B) as b:
                deviation(b * 2 + 1)
                act.wait_ge(s_scale, b * 2 + 1)
                act.wait_ge(row_out, PRIMED + b * T)
                nc.scalar.activation(halves(gp[0][:, 0, :]), parity(img[:, 0, :]), ACT.Identity,
                                     bias=sc[:, 9:10], scale=sc[:, 8:9])
                nc.scalar.activation(halves(g32), parity(img[:, 0, :]), ACT.Identity,
                                     bias=sc[:, 9:10], scale=sc[:, 8:9]).then_inc(g_done, 1)
                act.wait_ge(s_vscale, b + 1)
                act.wait_ge(uv_summed, PRIMED + (b + 1) * (T // 4))
                for dst in (halves(gp[1][0:NV, 0, :]), base0[0:NV]):
                    ins = nc.scalar.activation(dst, parity(uv_ps[0:NV, :]), ACT.Identity,
                                               bias=sc[0:NV, 13:14], scale=sc[0:NV, 12:13])
                ins.then_inc(vg_done, 1)
                act.wait_ge(vxt_made, b + 1)
                copy(xT[:, :, 0:NV], xt_ps[:, :, 0:NV]).then_inc(vxt_kept, 1)
                act.wait_ge(vh_made, b + 1)
                high_hilbert(1, NV).then_inc(vh_kept, 1)

                def normalise(n, t, s):
                    act.wait_ge(g_split, n)
                    nc.scalar.activation(halves(gp[s][:, 0, :]), parity(img[:, t, :]), ACT.Identity,
                                         bias=sc[:, 9:10], scale=sc[:, 8:9])
                    nc.scalar.activation(halves(g32), parity(img[:, t, :]), ACT.Identity,
                                         bias=sc[:, 9:10], scale=sc[:, 8:9]).then_inc(g_done, 1)

                def keep_turned(n):
                    act.wait_ge(xt_made, n + 1)
                    copy(xT, xt_ps[:]).then_inc(xt_kept, 1)

                def keep_hilbert(n, s):
                    act.wait_ge(h_made, n + 1)
                    high_hilbert(s).then_inc(h_kept, 1)

                def keep_base(n):
                    act.wait_ge(p0_ready, PRIMED + n + 1)
                    act.wait_ge(edge_kept, PRIMED + n + 1)
                    act.wait_ge(x1_done, PRIMED + n)
                    for a in range(2):
                        ins = nc.scalar.activation(base0[:, a, :], p0[:, a * HALF:(a + 1) * HALF], ACT.Identity,
                                                   bias=edge[:, 6 + a:7 + a], scale=unscale)
                    ins.then_inc(base_done, 1)

                keep_turned(b * T)
                act.wait_ge(v_mixed, b + 1)
                normalise(b * T + 1, 1, 1)
                keep_hilbert(b * T, 0)
                act.wait_ge(v_spread, b + 1)
                copy(rmap[:, 2], halves(p2[:])).then_inc(v_map_sin, 1)
                with act.Fori(0, T // 2 - 1) as i:
                    for s in range(2):
                        n = b * T + i * 2 + s
                        keep_turned(n + 1)
                        act.wait_ge(g_used, n + 1)
                        normalise(n + 2, i * 2 + (s + 2), s)
                        keep_base(n)
                        keep_hilbert(n + 1, 1 - s)
                keep_turned(b * T + T - 1)
                keep_base(b * T + T - 2)
                keep_hilbert(b * T + T - 1, 1)
                keep_base(b * T + T - 1)

                deviation(b * 2 + 2)
                act.wait_ge(s_scale, b * 2 + 2)
                act.wait_ge(pads_zero, b + 1)

                def pad_row(t, s, bias_row):
                    if not isinstance(t, int) or t >= 2:
                        act.wait_ge(row_summed, b * T + t - 1)
                    for a, bank in enumerate((p0, p1)):
                        act.wait_ge(col_summed[a], b * T + t + 1)
                        nc.scalar.activation(padded[s][:, K + a * HALF:K + (a + 1) * HALF], bank[:, 0:HALF],
                                             ACT.Identity, bias=box_bias[:, bias_row:bias_row + 1],
                                             scale=sc[:, 10:11]).then_inc(row_padded[a], 1)

                for t in range(R + 1):
                    pad_row(t, t % 2, t)
                with act.Fori((R + 1) // 2, (T - R - 1) // 2) as i:
                    for s in range(2):
                        pad_row(i * 2 + s, s, R)
                for t in range(T - R - 1, T):
                    pad_row(t, t % 2, t - (T - 2 * (R + 1)))

        @block.vector
        def _(dve):
            V = nc.vector
            count = [0]

            def link(ins, s=setup_chain):
                count[0] += 1
                ins.then_inc(s, 1)
                dve.wait_ge(s, count[0])

            dve.sem_inc(uv_summed, PRIMED)
            V.memset(sc[:], 0.0)
            V.memset(flat[:, 0:4 * 144], 0.0)
            V.memset(spaced, 0.0).then_inc(zeroed, 1)
            dve.wait_ge(zeroed, 1)
            dve.wait_ge(tab_in, 16 * len(TABLES))
            dve.wait_ge(w_in, 16 * (2 * (HB + 3) + 2))
            V.tensor_reduce(sc[:, 0:1], flat[:, 0:2 * 144], mybir.AxisListType.X, ALU.max,
                            apply_absolute_value=True).then_inc(max_w, 1)
            dve.wait_ge(max_all, 1)
            link(V.tensor_scalar(sc[:, 2:3], sc[:, 1:2], 1e-30, None, ALU.max))
            link(V.tensor_scalar(unscale, sc[:, 2:3], 1.0 / (MAT_SCALE * ROW_SCALE), None, ALU.mult))
            link(V.reciprocal(sc[:, 3:4], sc[:, 2:3]))
            link(V.tensor_scalar(flat[:, 0:4 * 144], flat[:, 0:4 * 144], sc[:, 3:4], MAT_SCALE, ALU.mult, ALU.mult))
            link(V.tensor_scalar(tb["cosw"][:], tb["cosw"][:], unscale, None, ALU.mult))
            wr, wi = raw
            link(V.tensor_copy(aa[:, 0, 0], wr[:, :, 1]))
            link(V.tensor_copy(aa[:, 1, 0], wi[:, :, 1]))
            link(V.tensor_tensor(aa[:, 0, 1], wr[:, :, 0], wr[:, :, 2], ALU.add))
            link(V.tensor_tensor(aa[:, 1, 1], wi[:, :, 0], wi[:, :, 2], ALU.add))
            link(V.tensor_tensor(aa[:, 0, 2], wi[:, :, 0], wi[:, :, 2], ALU.subtract))
            link(V.tensor_tensor(aa[:, 1, 2], wr[:, :, 2], wr[:, :, 0], ALU.subtract))
            ar, ai = aa[:, 0], aa[:, 1]

            def combine(dst, re, im, sr, si):
                def pair(j, a, op, sign):
                    if sign > 0 or op == ALU.subtract:
                        u, v = (0, 2) if sign > 0 else (2, 0)
                        link(V.tensor_tensor(dst(j), a[..., u], a[..., v], op))
                    else:
                        link(V.scalar_tensor_tensor(dst(j), a[..., 0], -1.0, a[..., 2], ALU.mult, ALU.subtract))
                link(V.tensor_scalar(dst(0), re[..., 1], float(sr), None, ALU.mult))
                link(V.tensor_scalar(dst(1), im[..., 1], float(-si), None, ALU.mult))
                pair(2, re, ALU.add, sr)
                pair(3, im, ALU.add, -si)
                pair(4, im, ALU.subtract, si)
                pair(5, re, ALU.subtract, sr)

            combine(lambda j: base[:, :, j], ar, ai, 1, 1)
            dve.sem_inc(base_ready, 1)
            row_matrices(V, link, scratch, range(0, 4))
            for blk, krow, col, swap, sr, si in ((0, 0, 1, False, 1, 1), (0, 0, 2, True, 1, -1),
                                                 (1, 2, 0, False, 1, 1), (2, 2, 0, True, -1, 1)):
                rows = slice(32 * blk, 32 * blk + C)
                re, im = (a[rows, :, krow] for a in (vraw[::-1] if swap else vraw))
                combine(lambda j: spaced[rows, j, col * C:(col + 1) * C], re, im, sr, si)
            link(V.tensor_copy(spaced16[:, 0:6], spaced))
            V.tensor_tensor(spaced16[:, 6:12], spaced, spaced16[:, 0:6], ALU.subtract).then_inc(vmat_spaced, 1)
            link(V.tensor_scalar(bias_row[:], bias_row[:], bcol[:, 1:2], -1.0, ALU.mult, ALU.mult))
            link(V.tensor_tensor(bias_row[:, 0:1], bias_row[:, 0:1], bcol[:, 0:1], ALU.add))
            for primed in (t1_done, t2_done, x1_done, xt_kept, terms_added, p0_ready, qx_done,
                           h_split, base_done, edge_kept,
                           row_out, *stored):
                dve.sem_inc(primed, PRIMED)
            def count_rows(b, k, r):
                dve.wait_ge(loaded[k], b * 16 + 16)
                V.bn_stats(stat[:, r + k * CHUNK, :], img[:, r + k * CHUNK, :]).then_inc(rows_counted, 1)
            for k in range(1, NCH // 2):
                for r in range(CHUNK):
                    count_rows(0, k, r)
            dve.wait_ge(pool_matrices, 6 * 2)
            V.memset(sc[:, 16:17], 0.0).then_inc(setup_done, 1)

            links = [0]

            def statistics(n, b):
                def lk(ins):
                    links[0] += 1
                    ins.then_inc(chain, 1)
                    dve.wait_ge(chain, b * LINKS + links[0])
                V.memset(sc[:, 19:20], 0.0)
                V.bn_aggr(sc[:, 0:2], stat[:].rearrange("p t s -> p (t s)")).then_inc(s_mean, 1)
                dve.wait_ge(s_gmean, n)
                dve.wait_ge(s_mean, n)
                lk(V.tensor_copy(sc[:, 6:7], c_ps[:, 16:17]))
                lk(V.tensor_tensor(sc[:, 2:3], sc[:, 0:1], sc[:, 6:7], ALU.subtract))
                V.scalar_tensor_tensor(sc[:, 3:4], sc[:, 2:3], sc[:, 2:3], sc[:, 1:2],
                                       ALU.mult, ALU.add).then_inc(s_dev, 1)
                dve.wait_ge(s_gvar, n)
                V.tensor_scalar(sc[:, 4:5], c_ps[:, 17:18], EPS, None, ALU.add).then_inc(s_var, 1)
                dve.wait_ge(s_sd, n)
                dve.wait_ge(s_var, n)
                lk(V.reciprocal(sc[:, 7:8], sc[:, 5:6]))
                lk(V.scalar_tensor_tensor(sc[:, 11:12], sc[:, 7:8], sc[:, 7:8], sc[:, 4:5], ALU.mult, ALU.mult))
                lk(V.tensor_scalar(sc[:, 11:12], sc[:, 11:12], -0.5, 1.5, ALU.mult, ALU.add))
                lk(V.tensor_tensor(sc[:, 7:8], sc[:, 7:8], sc[:, 11:12], ALU.mult))
                lk(V.tensor_scalar(sc[:, 8:9], sc[:, 7:8], ROW_SCALE, None, ALU.mult))
                lk(V.scalar_tensor_tensor(sc[:, 9:10], sc[:, 8:9], -1.0, sc[:, 6:7], ALU.mult, ALU.mult))
                lk(V.tensor_scalar(sc[:, 10:11], sc[:, 7:8], 1.0 / (K * K), None, ALU.mult))
                lk(V.scalar_tensor_tensor(sc[:, 14:15], sc[:, 10:11], -1.0, sc[:, 6:7], ALU.mult, ALU.mult))
                V.tensor_scalar(box_bias[:], tb["row_count"][:], sc[:, 14:15], None,
                                ALU.mult).then_inc(s_scale, 1)

            LINKS = 2 * 10 + 5

            def layer0(b):
                links[0] = 0

                def lk(ins):
                    links[0] += 1
                    ins.then_inc(chain, 1)
                    dve.wait_ge(chain, b * LINKS + links[0])

                dve.wait_ge(rows_counted, (b + 1) * T)
                statistics(b * 2 + 1, b)
                dve.wait_ge(s_vsum, b + 1)
                V.tensor_copy(sc[0:NV, 12:13], c_ps[0:NV, 18:19])
                V.memset(sc[:, 13:14], 0.0)
                lk(V.memset(sc[:, 15:16], 0.0))
                V.tensor_copy(sc[0:C, 13:14], c_ps[0:C, 19:20]).then_inc(s_vscale, 1)

                def spread(t, s):
                    V.tensor_tensor(bd[s], smat[:, t, :, :].unsqueeze(2).broadcast_to([P, 12, HB, C]),
                                    tb["hb_mask16"][:].unsqueeze(1).broadcast_to([P, 12, HB, C]),
                                    ALU.mult).then_inc(bd_ready, 1)

                def split_h(s, kept, done, n, rows=P):
                    dve.wait_ge(kept, n + 1)
                    V.scalar_tensor_tensor(hp[s][0:rows, 1, :, 0:HALF + NZ], h_ps[0:rows, :, 0:HALF + NZ],
                                           1.0 / TAB_SCALE, hp[s][0:rows, 0, :, 0:HALF + NZ],
                                           ALU.mult, ALU.subtract).then_inc(done, 1)

                for s in range(NS):
                    dve.wait_ge(stored[s], PRIMED + b * (16 * T // (2 * NS)))
                dve.wait_ge(vg_done, b + 1)
                V.tensor_tensor(halves(gp[1][0:NV, 1, :]), base0[0:NV], halves(gp[1][0:NV, 0, :]),
                                ALU.subtract).then_inc(vg_split, 1)
                spread(0, 0)
                split_h(1, vh_kept, vh_split, b, NV)
                spread(1, 1)
                dve.wait_ge(g_done, b * T + 1)
                V.tensor_tensor(img[:, 0, :], img[:, 0, :], bias_row[:], ALU.add).then_inc(bias_added, 1)
                dve.wait_ge(v_mixed, b + 1)

                def term(dst, pt, cc, wave, rows):
                    for a in range(2):
                        ins = V.scalar_tensor_tensor(dst[0:rows, a, :], pt[0:rows, a * HALF:(a + 1) * HALF],
                                                     edge[0:rows, cc + a:cc + a + 1], wave[0:rows, a, :],
                                                     ALU.add, ALU.mult)
                    return ins
                lk(V.tensor_copy(edge[0:NV, 0:6], c_ps[0:NV, 0:6]))
                term(t1, p1, 4, cosw, NV)
                lk(term(t2, p2, 0, sinw, NV))
                lk(V.tensor_tensor(t1[0:NV], t1[0:NV], t2[0:NV], ALU.add))
                for a in range(2):
                    ins = V.tensor_scalar(base0[0:NV, a, :], p0[0:NV, a * HALF:(a + 1) * HALF],
                                          edge[0:NV, 2 + a:3 + a], unscale[0:NV], ALU.add, ALU.mult)
                lk(ins)
                V.tensor_tensor(qx[0:NV], base0[0:NV], t1[0:NV], ALU.add).then_inc(v_rows, 1)
                dve.wait_ge(v_spread, b + 1)
                for j, pt in enumerate((p0, p1)):
                    ins = V.tensor_copy(rmap[:, j], halves(pt[:]))
                ins.then_inc(v_maps, 1)
                dve.wait_ge(v_maps, b + 1)
                assert links[0] <= LINKS

                def wrap_first(t, s):
                    V.scalar_tensor_tensor(wadd[s], rmap[:, 1], tb["trig_h"][:, 0, bass.ds(t, 1)], rmap[:, 0],
                                           ALU.mult, ALU.add).then_inc(wrap_begun, 1)

                def wrap_second(n, t, s):
                    dve.wait_ge(wrap_begun, n + 1)
                    V.scalar_tensor_tensor(wadd[s], rmap[:, 2], tb["trig_h"][:, 1, bass.ds(t, 1)], wadd[s],
                                           ALU.mult, ALU.add).then_inc(wrap_done, 1)

                def keep_edge(n):
                    dve.wait_ge(edge_ready, n + 1)
                    dve.wait_ge(base_done, PRIMED + n)
                    V.tensor_copy(edge[:, 0:6], c_ps[:, 0:6])
                    V.tensor_scalar(edge[:, 6:8], c_ps[:, 2:4], unscale, None, ALU.mult).then_inc(edge_kept, 1)

                def row(n, t, s, spread_ahead=True, more_rows=True):
                    dve.wait_ge(edge_kept, PRIMED + n + 1)
                    dve.wait_ge(p1_ready, n + 1)
                    dve.wait_ge(terms_added, PRIMED + n)
                    term(t1, p1, 4, cosw, P).then_inc(t1_done, 1)
                    dve.wait_ge(p2_ready, n + 1)
                    term(t2, p2, 0, sinw, P).then_inc(t2_done, 1)
                    if more_rows:
                        wrap_first(t + 1, 1 - s)
                        split_h(1 - s, h_kept, h_split, n + 1)
                        wrap_second(n + 1, t + 1, 1 - s)
                    if spread_ahead:
                        dve.wait_ge(p0_ready, PRIMED + n + 1)
                        spread(t + 2, s)
                    dve.wait_ge(base_done, PRIMED + n + 1)
                    dve.wait_ge(terms_added, PRIMED + n + 1)
                    V.tensor_tensor(parity(img[:, t, :]), base0[:], qx, ALU.add).then_inc(x1_done, 1)
                    if more_rows:
                        keep_edge(n + 1)
                    dve.wait_ge(x1_done, PRIMED + n + 1)
                    V.bn_stats(stat[:, t, :], img[:, t, :]).then_inc(x1_counted, 1)

                dve.wait_ge(qx_done, PRIMED + b * T)
                wrap_first(0, 0)
                dve.wait_ge(v_map_sin, b + 1)
                wrap_second(b * T, 0, 0)
                split_h(0, h_kept, h_split, b * T)
                keep_edge(b * T)
                with dve.Fori(0, T // 2 - 1) as i:
                    for s in range(2):
                        row(b * T + i * 2 + s, i * 2 + s, s)
                row(b * T + T - 2, T - 2, 0, spread_ahead=False)
                row(b * T + T - 1, T - 1, 1, spread_ahead=False, more_rows=False)
                dve.wait_ge(x1_counted, (b + 1) * T)
                statistics(b * 2 + 2, b)
                assert links[0] == LINKS, links[0]

            def layer1(b, follow):
                for s in range(2):
                    V.memset(padded[s][:, 0:K], 0.0)
                    ins = V.memset(padded[s][:, K + W:PADW], 0.0)
                ins.then_inc(pads_zero, 1)
                dve.wait_ge(pads_zero, b + 1)

                def run_sum(n, s):
                    dve.wait_ge(row_padded[0], n + 1)
                    dve.wait_ge(row_padded[1], n + 1)
                    V.tensor_tensor_scan(sums[s], padded[s][:, K:K + SUMW], padded[s][:, 0:SUMW], 0.0,
                                         ALU.add, ALU.subtract).then_inc(row_summed, 1)

                def difference(t, s):
                    dve.wait_ge(col_summed[1], b * T + t)
                    V.tensor_tensor(diff[s], img[:, t + (R + 1), :], img[:, t - R, :],
                                    ALU.subtract).then_inc(moved, 1)

                def steps(lo, hi, diffs):
                    with dve.Fori(lo // 2, hi // 2) as i:
                        for s in range(2):
                            dve.wait_ge(row_out, PRIMED + b * T + i * 2 + (s - 1))
                            run_sum(b * T + i * 2 + s, s)
                            if diffs:
                                difference(i * 2 + (s + 2), s)

                for s in range(2):
                    run_sum(b * T + s, s)
                steps(2, R - 1, False)
                difference(R, 1)
                steps(R - 1, T // 2, True)
                for q in range(AHEAD):
                    for r in range(CHUNK):
                        t = T - CHUNK * (AHEAD - q) + r
                        dve.wait_ge(row_out, PRIMED + b * T + t - 1)
                        run_sum(b * T + t, t % 2)
                        if t + 2 < T - R - 1:
                            difference(t + 2, t % 2)
                        if follow:
                            count_rows(b + 1, q + 1, r)
                if follow:
                    for k in [*range(AHEAD + 1, NCH), 0]:
                        for r in range(CHUNK):
                            count_rows(b + 1, k, r)

            for k in [*range(NCH // 2, NCH), 0]:
                for r in range(CHUNK):
                    count_rows(0, k, r)
            with dve.Fori(0, B - 1) as b:
                layer0(b)
                layer1(b, True)
            layer0(B - 1)
            layer1(B - 1, False)

        @block.gpsimd
        def _(pool):
            G = nc.gpsimd
            pool.wait_ge(max_w, 1)
            G.partition_all_reduce(sc[:, 1:2], sc[:, 0:1], P, bass.bass_isa.ReduceOp.max).then_inc(max_all, 1)
            pool.wait_ge(tab_in, 16 * len(TABLES))

            def sum_weights(b, q, s):
                if q == 0:
                    pool.wait_ge(uv_summed, PRIMED + b * (T // 4))
                else:
                    pool.wait_ge(uv_summed, PRIMED + b * (T // 4) + (2 * q + s - 1))
                t = (q + 1) % NCH * CHUNK + 4 * s
                rows = tb["virt_h"][:, t:t + 4, :].rearrange("p t j -> p (t j)")
                G.tensor_tensor(uvw[s][:, :, 0:C], rows.unsqueeze(2).broadcast_to([P, 12, C]),
                                tb["c_mask"][:].unsqueeze(1).broadcast_to([P, 12, C]),
                                ALU.mult).then_inc(uvw_ready, 1)

            pool.wait_ge(base_ready, 1)
            made = [0]

            def link(ins):
                made[0] += 1
                ins.then_inc(pool_matrices, 1)
                sum_weights(0, (made[0] - 1) // 2, (made[0] - 1) % 2)
                pool.wait_ge(pool_matrices, made[0])
            row_matrices(G, link, scratch_g, range(4, 6))
            pool.wait_ge(setup_done, 1)

            def layer0(b):
                def split_g(n, s):
                    pool.wait_ge(g_done, n + 1)
                    G.tensor_tensor(gp[s][:, 1, :], g32, gp[s][:, 0, :], ALU.subtract).then_inc(g_split, 1)

                def add_row(n, t, s):
                    pool.wait_ge(wrap_done, n + 1)
                    pool.wait_ge(x1_done, PRIMED + n)
                    G.tensor_tensor(qx, wadd[s], parity(img[:, t, :]), ALU.add).then_inc(qx_done, 1)

                def add_terms(n):
                    pool.wait_ge(t1_done, PRIMED + n + 1)
                    pool.wait_ge(qx_done, PRIMED + n + 1)
                    G.tensor_tensor(qx, qx, t1, ALU.add).then_inc(t1_added, 1)
                    pool.wait_ge(t2_done, PRIMED + n + 1)
                    pool.wait_ge(t1_added, n + 1)
                    G.tensor_tensor(qx, qx, t2, ALU.add).then_inc(terms_added, 1)

                split_g(b * T, 0)
                pool.wait_ge(bias_added, b + 1)
                split_g(b * T + 1, 1)
                with pool.Fori(0, T // 2 - 1) as i:
                    for s in range(2):
                        n = b * T + i * 2 + s
                        split_g(n + 2, s)
                        add_row(n, i * 2 + s, s)
                        add_terms(n)
                for s in range(2):
                    add_row(b * T + T - 2 + s, T - 2 + s, s)
                    add_terms(b * T + T - 2 + s)

            def layer1(b, follow):
                def two_rows(i, s):
                    pool.wait_ge(stored[s], PRIMED + (b * (T // (2 * NS)) + i) * 16)
                    for r in range(2):
                        t = i * (2 * NS) + (2 * s + r)
                        pool.wait_ge(row_summed, b * T + t + 1)
                        G.tensor_tensor(ob[s][:, r, :], sums[r][:, R:R + W], img[:, t, :],
                                        ALU.add).then_inc(row_out, 1)

                with pool.Fori(0, T // 2 // (2 * NS)) as i:
                    for s in range(NS):
                        two_rows(i, s)
                if follow:
                    for s in range(2):
                        sum_weights(b + 1, 0, s)
                for j in range(T // 8, T // 4):
                    for s in range(2):
                        two_rows(j // 2, 2 * (j % 2) + s)
                    if follow:
                        q, s = divmod(j - T // 8 + 2, 2)
                        sum_weights(b + 1, q, s)
                if follow:
                    for j in range(2 * AHEAD + 2, 2 * NCH):
                        sum_weights(b + 1, j // 2, j % 2)

            for q in range(made[0] // 2, NCH):
                for s in range(2):
                    sum_weights(0, q, s)
            with pool.Fori(0, B - 1) as b:
                layer0(b)
                layer1(b, True)
            layer0(B - 1)
            layer1(B - 1, False)


_INS = ["x", "L0_conv_w_real", "L0_conv_w_imag", "L0_conv_b_real", "L0_conv_b_imag"]


def kernel(**inputs):
    import concourse.bacc as bacc
    from concourse.bass_utils import run_bass_kernel_spmd

    nc = bacc.Bacc("TRN2", target_bir_lowering=False, num_devices=1)
    arrays, args = {}, []
    for name in _INS:
        a = np.ascontiguousarray(inputs[name])
        arrays[f"in_{name}"] = a
        args.append(nc.dram_tensor(f"in_{name}", a.shape, mybir.dt.from_np(a.dtype), kind="ExternalInput").ap())
    tab = {}
    for name, a in tables().items():
        arrays[f"tab_{name}"] = a
        tab[name] = nc.dram_tensor(f"tab_{name}", a.shape, mybir.dt.from_np(a.dtype), kind="ExternalInput").ap()
    out = nc.dram_tensor("out_0", (B, C, H, W), F32, kind="ExternalOutput").ap()
    build(nc, *args, tab, out)
    r = run_bass_kernel_spmd(nc, [arrays], core_ids=[0])
    return r.results[0]["out_0"]
```
